# Optimizing a Trainium2 kernel written in Bass

```python
import numpy as np
import jax
import jax.numpy as jnp

def _softmax(x, axis=-1):
    return jax.nn.softmax(x, axis=axis)

def _gelu(x):
    return jax.nn.gelu(x, approximate=True)

def _silu(x):
    return jax.nn.silu(x)

def _sigmoid(x):
    return jax.nn.sigmoid(x)

def _layernorm(x, axis=-1, eps=1e-05):
    m = jnp.mean(x, axis=axis, keepdims=True)
    v = jnp.var(x, axis=axis, keepdims=True)
    return (x - m) / jnp.sqrt(v + eps)

def _scatter_add(tgt, idx, src, axis=0):
    return tgt.at[idx].add(src)

def _segment_sum(src, seg, n):
    return jax.ops.segment_sum(src, seg, n)
kernel_name = 'mk_xattn_seq_d1_seqx_r4_6362f5'

def setup_inputs(seed: int=0):
    np.random.seed(seed)
    _w = jnp.asarray

    def _rec_inputs():
        import jax
        import jax.numpy as jnp
        _rk = jax.random.key(seed)
        x = -0.0001233 + 1 * jax.random.normal(jax.random.fold_in(_rk, 1), (16, 112, 320), jnp.float32)
        _lenS = 112 - jax.random.randint(jax.random.fold_in(_rk, 7), (16,), 0, max(1, 112 // 4) + 1, jnp.int32)
        _lenS2 = 375 - jax.random.randint(jax.random.fold_in(_rk, 8), (16,), 0, max(1, 375 // 4) + 1, jnp.int32)
        _ctx_768P = jax.random.normal(jax.random.fold_in(_rk, 11), (16, 16, 192), jnp.float32)
        _ctx_768c = jax.random.dirichlet(jax.random.fold_in(_rk, 511), 0.3 * jnp.ones((16,), jnp.float32), (16, 375))
        _ctx_768t = jnp.einsum('bsk,bkd->bsd', _ctx_768c, _ctx_768P)
        _ctx_768t = _ctx_768t * jax.lax.rsqrt(jnp.mean(jnp.square(_ctx_768t)) + 1e-12) * 0.953939
        ctx_768 = 0.00272024 + 0.999456 * (_ctx_768t + 0.3 * jax.random.normal(jax.random.fold_in(_rk, 611), (16, 375, 192), jnp.float32))
        return (x, ctx_768)
    x, ctx_768 = _rec_inputs()

    def _L0_xattn_setup():
        import jax, jax.numpy as jnp
        import numpy as np
        D = 320
        H = 20
        DH = D // H
        CTX = 192
        FF_IN = 4 * D
        EPS = 1e-05

        def _ln(x, g, b):
            m = jnp.mean(x, axis=-1, keepdims=True)
            v = jnp.mean(jnp.square(x - m), axis=-1, keepdims=True)
            return (x - m) * jax.lax.rsqrt(v + EPS) * g + b

        def _attn(x, ctx, wq, wk, wv, wo, bo, heads):
            b, n, _ = x.shape
            j = ctx.shape[1]
            dh = wq.shape[1] // heads
            scale = dh ** (-0.5)
            q = (x @ wq).reshape(b, n, heads, dh).transpose(0, 2, 1, 3)
            k = (ctx @ wk).reshape(b, j, heads, dh).transpose(0, 2, 1, 3)
            v = (ctx @ wv).reshape(b, j, heads, dh).transpose(0, 2, 1, 3)
            sim = jnp.einsum('bhid,bhjd->bhij', q, k) * scale
            a = jax.nn.softmax(sim, axis=-1)
            out = jnp.einsum('bhij,bhjd->bhid', a, v)
            out = out.transpose(0, 2, 1, 3).reshape(b, n, heads * dh)
            return out @ wo + bo
        key = jax.random.key(seed)
        ks = jax.random.split(key, 24)
        r = lambda k, shp, s: jax.random.normal(k, shp, dtype=jnp.float32) * s
        d = {'x': r(ks[0], (8, 256, D), 1.0), 'context': r(ks[1], (8, 77, CTX), 1.0), 'heads': H, 'n1_g': jnp.ones((D,), jnp.float32), 'n1_b': jnp.zeros((D,), jnp.float32), 'q1': r(ks[2], (D, D), D ** (-0.5)), 'k1': r(ks[3], (D, D), D ** (-0.5)), 'v1': r(ks[4], (D, D), D ** (-0.5)), 'o1_w': r(ks[5], (D, D), D ** (-0.5)), 'o1_b': jnp.zeros((D,), jnp.float32), 'n2_g': jnp.ones((D,), jnp.float32), 'n2_b': jnp.zeros((D,), jnp.float32), 'q2': r(ks[6], (D, D), D ** (-0.5)), 'k2': r(ks[7], (CTX, D), CTX ** (-0.5)), 'v2': r(ks[8], (CTX, D), CTX ** (-0.5)), 'o2_w': r(ks[9], (D, D), D ** (-0.5)), 'o2_b': jnp.zeros((D,), jnp.float32), 'n3_g': jnp.ones((D,), jnp.float32), 'n3_b': jnp.zeros((D,), jnp.float32), 'ff_w1': r(ks[10], (D, 2 * FF_IN), D ** (-0.5)), 'ff_b1': jnp.zeros((2 * FF_IN,), jnp.float32), 'ff_w2': r(ks[11], (FF_IN, D), FF_IN ** (-0.5)), 'ff_b2': jnp.zeros((D,), jnp.float32)}
        return d
    _L0_xattn_all = _L0_xattn_setup()
    _L0_xattn_in = {k: v for k, v in _L0_xattn_all.items() if k in ('n1_g', 'n1_b', 'q1', 'k1', 'v1', 'o1_w', 'o1_b', 'n2_g', 'n2_b', 'q2', 'k2', 'v2', 'o2_w', 'o2_b', 'n3_g', 'n3_b', 'ff_w1', 'ff_b1', 'ff_w2', 'ff_b2')}
    del _L0_xattn_all
    return {'x': x, 'ctx_768': ctx_768, 'L0_xattn_n1_g': _L0_xattn_in['n1_g'], 'L0_xattn_n1_b': _L0_xattn_in['n1_b'], 'L0_xattn_q1': _L0_xattn_in['q1'], 'L0_xattn_k1': _L0_xattn_in['k1'], 'L0_xattn_v1': _L0_xattn_in['v1'], 'L0_xattn_o1_w': _L0_xattn_in['o1_w'], 'L0_xattn_o1_b': _L0_xattn_in['o1_b'], 'L0_xattn_n2_g': _L0_xattn_in['n2_g'], 'L0_xattn_n2_b': _L0_xattn_in['n2_b'], 'L0_xattn_q2': _L0_xattn_in['q2'], 'L0_xattn_k2': _L0_xattn_in['k2'], 'L0_xattn_v2': _L0_xattn_in['v2'], 'L0_xattn_o2_w': _L0_xattn_in['o2_w'], 'L0_xattn_o2_b': _L0_xattn_in['o2_b'], 'L0_xattn_n3_g': _L0_xattn_in['n3_g'], 'L0_xattn_n3_b': _L0_xattn_in['n3_b'], 'L0_xattn_ff_w1': _L0_xattn_in['ff_w1'], 'L0_xattn_ff_b1': _L0_xattn_in['ff_b1'], 'L0_xattn_ff_w2': _L0_xattn_in['ff_w2'], 'L0_xattn_ff_b2': _L0_xattn_in['ff_b2']}

def reference(x, ctx_768, L0_xattn_n1_g, L0_xattn_n1_b, L0_xattn_q1, L0_xattn_k1, L0_xattn_v1, L0_xattn_o1_w, L0_xattn_o1_b, L0_xattn_n2_g, L0_xattn_n2_b, L0_xattn_q2, L0_xattn_k2, L0_xattn_v2, L0_xattn_o2_w, L0_xattn_o2_b, L0_xattn_n3_g, L0_xattn_n3_b, L0_xattn_ff_w1, L0_xattn_ff_b1, L0_xattn_ff_w2, L0_xattn_ff_b2):
    import jax
    import jax.numpy as jnp

    def _L0_xattn_ref(x, context, heads, n1_g, n1_b, q1, k1, v1, o1_w, o1_b, n2_g, n2_b, q2, k2, v2, o2_w, o2_b, n3_g, n3_b, ff_w1, ff_b1, ff_w2, ff_b2):
        import jax, jax.numpy as jnp
        import numpy as np
        D = 320
        H = 20
        DH = D // H
        CTX = 192
        FF_IN = 4 * D
        EPS = 1e-05

        def _ln(x, g, b):
            m = jnp.mean(x, axis=-1, keepdims=True)
            v = jnp.mean(jnp.square(x - m), axis=-1, keepdims=True)
            return (x - m) * jax.lax.rsqrt(v + EPS) * g + b

        def _attn(x, ctx, wq, wk, wv, wo, bo, heads):
            b, n, _ = x.shape
            j = ctx.shape[1]
            dh = wq.shape[1] // heads
            scale = dh ** (-0.5)
            q = (x @ wq).reshape(b, n, heads, dh).transpose(0, 2, 1, 3)
            k = (ctx @ wk).reshape(b, j, heads, dh).transpose(0, 2, 1, 3)
            v = (ctx @ wv).reshape(b, j, heads, dh).transpose(0, 2, 1, 3)
            sim = jnp.einsum('bhid,bhjd->bhij', q, k) * scale
            a = jax.nn.softmax(sim, axis=-1)
            out = jnp.einsum('bhij,bhjd->bhid', a, v)
            out = out.transpose(0, 2, 1, 3).reshape(b, n, heads * dh)
            return out @ wo + bo
        h1 = _ln(x, n1_g, n1_b)
        x = _attn(h1, h1, q1, k1, v1, o1_w, o1_b, heads) + x
        h2 = _ln(x, n2_g, n2_b)
        x = _attn(h2, context, q2, k2, v2, o2_w, o2_b, heads) + x
        h3 = _ln(x, n3_g, n3_b)
        proj = h3 @ ff_w1 + ff_b1
        a, g = jnp.split(proj, 2, axis=-1)
        ff = a * jax.nn.gelu(g, approximate=False) @ ff_w2 + ff_b2
        return ff + x
    x = _L0_xattn_ref(x, ctx_768, 20, L0_xattn_n1_g, L0_xattn_n1_b, L0_xattn_q1, L0_xattn_k1, L0_xattn_v1, L0_xattn_o1_w, L0_xattn_o1_b, L0_xattn_n2_g, L0_xattn_n2_b, L0_xattn_q2, L0_xattn_k2, L0_xattn_v2, L0_xattn_o2_w, L0_xattn_o2_b, L0_xattn_n3_g, L0_xattn_n3_b, L0_xattn_ff_w1, L0_xattn_ff_b1, L0_xattn_ff_w2, L0_xattn_ff_b2)
    return x

_drawn_inputs = setup_inputs


def setup_inputs(seed=0):
    import zlib

    import numpy as np

    out = dict(_drawn_inputs(seed))
    spreads = {'L0_xattn_n1_g': (1.0, 0.2),
     'L0_xattn_n1_b': (0.0, 0.1),
     'L0_xattn_o1_b': (0.0, 0.1),
     'L0_xattn_n2_g': (1.0, 0.2),
     'L0_xattn_n2_b': (0.0, 0.37),
     'L0_xattn_o2_b': (0.0, 0.1),
     'L0_xattn_n3_g': (1.0, 0.2),
     'L0_xattn_n3_b': (0.0, 0.1),
     'L0_xattn_ff_b1': (0.0, 0.1),
     'L0_xattn_ff_b2': (0.0, 0.1)}
    factors = {}
    for name, (base, spread) in spreads.items():
        noise = np.random.default_rng([zlib.crc32(name.encode()), seed]).standard_normal(out[name].shape)
        drawn = base * np.exp(spread * noise) if base else spread * noise
        out[name] = jnp.asarray(drawn.astype(out[name].dtype))
    for name, factor in factors.items():
        out[name] = (out[name] * factor).astype(out[name].dtype)
    return out
```

```python
from contextlib import ExitStack

import concourse.bass as bass
from concourse import mybir

ALU = mybir.AluOpType
ACT = mybir.ActivationFunctionType
AX = mybir.AxisListType
F32 = mybir.dt.float32
F32R = mybir.dt.float32r
BF16 = mybir.dt.bfloat16

B, N, D = 16, 112, 320
H, DH = 20, 16
CTX, J = 192, 375
JP = J + 1
F = 4 * D
PAIRS = B // 2
T = 2 * N
HG = H // 4
JT, JW = 3, J // 3
KT = 3
FT = F // 128
STACK = 6 * DH
VW = DH + 1
EPS = 1e-05
SCALE = DH ** -0.5

PASSES_D = [(0, 0, 128), (1, 0, 128), (0, 1, 128), (2, 2, 128), (3, 2, 128), (2, 3, 128),
            (4, 4, 128), (5, 4, 64)]
PASSES_C = [(0, 0, 128), (1, 0, 128), (0, 1, 128), (2, 2, 128), (3, 2, 64)]
Q_PARTS = [0, 0, 0, 1, 1, 2]
K_PARTS = [0, 1, 2, 0, 1, 0]



def r32(ap):
    return ap.bitcast(F32R)


class Signal:

    def __init__(self, ctx, nc, name, per, lead=1):
        self.sem = ctx.enter_context(nc.semaphore(name))
        self.per, self.lead = per, lead

    def at(self, p, k):
        if isinstance(p, tuple):
            p, offset = p
            k += offset * self.per
        return p * self.per + (k + self.lead)


class Loop:
    pass


class Norm:
    pass


class Weights:
    pass


class Ring:

    def __init__(self, ctx, nc, name, banks, parts):
        self.ready = Signal(ctx, nc, name + "_ready", 0)
        self.used = [Signal(ctx, nc, f"{name}_used{i}", 0) for i in range(len(banks))]
        self.banks = banks
        self.parts, start = {}, 0
        for kind, names, p0, count in parts:
            assert count == 1 or len(names) % len(banks) == 0
            self.parts[kind] = (start, names, p0)
            start += len(names) * count

    def number(self, at, name, every=1):
        kind, p = at
        start, names, p0 = self.parts[kind]
        n = (start + names.index(name)) // every
        return n if isinstance(p, int) and p == p0 else (p - p0) * (len(names) // every) + n

    def slot(self, at, name):
        start, names, _ = self.parts[at[0]]
        return (start + names.index(name)) % len(self.banks)

    def bank(self, at, name):
        return self.banks[self.slot(at, name)]

    def wait_free(self, eng, at, name):
        u = self.used[self.slot(at, name)]
        eng.wait_ge(u.sem, self.number(at, name, len(self.banks)) + u.lead)

    def wait_used(self, eng, at, name):
        u = self.used[self.slot(at, name)]
        eng.wait_ge(u.sem, self.number(at, name, len(self.banks)) + (1 + u.lead))

    def wait_ready(self, eng, at, name):
        eng.wait_ge(self.ready.sem, self.number(at, name) + (1 + self.ready.lead))

    def release(self, ins, at, name):
        ins.then_inc(self.used[self.slot(at, name)].sem, 1)


def build(nc, x, ctx_t, q1, k1, v1, o1, q2, k2, v2, o2, w1, w2, ln_cols, b1_cols, bias_rows, ident, out):
    top = ExitStack()
    with top:
        def dram(name, shape, dt):
            return nc.dram_tensor(name, shape, dt, kind="Internal").ap()

        qk_scr = dram("qk_scr", [PAIRS, 3, 2 * D, T], BF16)
        q2_scr = dram("q2_scr", [PAIRS, 3, D, T], BF16)
        k2_scr = dram("k2_scr", [B, 3, D, JP], BF16)
        v2_scr = dram("v2_scr", [B, JW, JT * H * VW], F32)
        x1_scr = dram("x1_scr", [B, N, D], F32)

        def sbt(ctx, name, shape, dt=F32):
            return ctx.enter_context(nc.sbuf_tensor(name, shape, dt))

        ps = top.enter_context(nc.psum_tensor("ps", [128, 8, 512], F32))
        eye = sbt(top, "eye", [128, 128])
        lnc = sbt(top, "lnc", [128, 3, KT, 2])
        b1c = sbt(top, "b1c", [128, 2 * FT])
        brow = sbt(top, "brow", [N, 3, D])
        neghalf = sbt(top, "neghalf", [N, 2])
        epsc = sbt(top, "epsc", [N, 2])

        const_loaded = Signal(top, nc, "const_loaded", 0, 0)

        def load_weights(sp, W, chunks, which):
            for i in which:
                kind, sources, w, c0, n = chunks[i]
                raw = W.raw[i]
                if i >= 2:
                    sp.wait_ge(W.lo.sem, i - 1)
                for src, at, m in sources:
                    if kind == "d":
                        views = [(raw[:, 0:2, at:at + m], src[0:256].rearrange("(k p) m -> p k m", p=128)),
                                 (raw[0:64, 2, at:at + m], src[256:320]), (raw[64:128, 2, at:at + m], src[256:320])]
                    elif kind == "c":
                        views = [(raw[:, 0, at:at + m], src[0:128]), (raw[0:64, 1, at:at + m], src[128:192]),
                                 (raw[64:128, 1, at:at + m], src[128:192])]
                    else:
                        flat = raw[:].rearrange("p a b -> p (a b)")[:, 0:n * D].rearrange("p (k m) -> p k m", m=D)
                        views = [(flat, src[c0 * 128:(c0 + n) * 128].rearrange("(k p) m -> p k m", p=128))]
                    for dst, s in views:
                        sp.dma_start(dst, s).then_inc(W.loaded[i].sem, 16)

        def split_hi(act, W, chunks, which):
            for i in which:
                kind, sources, w, c0, n = chunks[i]
                raw = W.raw[i]
                act.wait_ge(W.loaded[i].sem, 16 * len(sources) * (1 if kind == "f" else 3))
                if kind == "d":
                    ins = act.copy(r32(w[:, 0:5:2, c0:c0 + n]), raw[:, 0:3, 0:n])
                elif kind == "c":
                    ins = act.copy(r32(w[:, 0:3:2, c0:c0 + n]), raw[:, 0:2, 0:n])
                else:
                    flat = raw[:].rearrange("p a b -> p (a b)")[:, 0:n * D].rearrange("p (k m) -> p k m", m=D)
                    ins = act.copy(r32(w[:, c0:c0 + n, 0]), flat)
                ins.then_inc(W.hi.sem, 1)

        def split_lo(eng, W, chunks, which):
            for i in which:
                kind, _, w, c0, n = chunks[i]
                raw = W.raw[i]
                eng.wait_ge(W.hi.sem, i + 1)
                c = slice(c0, c0 + n)
                if kind == "d":
                    eng.tensor_tensor(r32(w[:, 1:4:2, c]), raw[:, 0:2, 0:n], w[:, 0:3:2, c], ALU.subtract)
                    ins = eng.tensor_tensor(r32(w[64:128, 4, c]), raw[64:128, 2, 0:n], w[64:128, 4, c], ALU.subtract)
                elif kind == "c":
                    eng.tensor_tensor(r32(w[:, 1, c]), raw[:, 0, 0:n], w[:, 0, c], ALU.subtract)
                    ins = eng.tensor_tensor(r32(w[64:128, 2, c]), raw[64:128, 1, 0:n], w[64:128, 2, c], ALU.subtract)
                else:
                    flat = raw[:].rearrange("p a b -> p (a b)")[:, 0:n * D].rearrange("p (k m) -> p k m", m=D)
                    ins = eng.tensor_tensor(r32(w[:, c, 1]), flat, w[:, c, 0], ALU.subtract)
                ins.then_inc(W.lo.sem, 1)

        def ln_stats(dve, L, n, p, s, src, batches):
            for b in batches:
                ins = dve.bn_stats(n.stats[:, b, :], src[:, b, :])
            ins.then_inc(n.stats_done.sem, 1)
            dve.wait_ge(n.stats_done.sem, n.stats_done.at(p, s + 1))
            dve.memset(L.tick[:], 0.0)
            for b in batches:
                ins = dve.bn_aggr(n.mv[:, b, :], n.stats[:, b, :])
            ins.then_inc(n.aggr_done.sem, 1)

        def ln_scale(dve, L, n, p, s, src, batches):
            dve.wait_ge(n.rstd_done.sem, n.rstd_done.at(p, s + 1))
            for b in batches:
                ins = dve.tensor_scalar(L.z[:, b, 0:D], src[:, b, :], n.mv[:, b, 0:1], n.rstd[:, b:b + 1],
                                        ALU.subtract, ALU.mult)
            ins.then_inc(n.z_done.sem, 1)

        def ln_rstd(pool, n, p, s, batches):
            c = slice(batches[0], batches[-1] + 1)
            pool.wait_ge(n.aggr_done.sem, n.aggr_done.at(p, s + 1))
            pool.tensor_tensor(n.ve[:, c], n.mv[:, c, 1], epsc[:, c], ALU.add).then_inc(n.var_done.sem, 1)
            pool.wait_ge(n.var_done.sem, n.var_done.at(p, s + 1))
            pool.tensor_tensor(n.rstd[:, c], n.ve[:, c], neghalf[:, c], ALU.pow).then_inc(n.rstd_done.sem, 1)

        def ln_turn(pe, L, n, p, at, uses):
            pe.wait_ge(n.z_done.sem, n.z_done.at(p, n.z_done.per))
            for use, tiles in zip(uses, [(0, 1), (2,)]):
                L.dense.wait_free(pe, at, use)
                bank = L.dense.bank(at, use)
                for kt in tiles:
                    for b in range(2):
                        c = (kt % 2) * T + b * N
                        mm = pe.transpose(ps[:, bank, c:c + N], L.z[:, b, 128 * kt:128 * kt + 128], eye[0:N, 0:N])
                mm.then_inc(L.dense.ready.sem, 1)

        def ln_hi(act, L, n, at, uses, hT, halves=range(2)):
            if 0 in halves:
                L.dense.wait_ready(act, at, uses[0])
                bank = L.dense.bank(at, uses[0])
                for kt in range(2):
                    ins = act.activation(r32(hT[:, 2 * kt, :]), ps[:, bank, kt * T:kt * T + T], ACT.Identity,
                                         scale=lnc[:, n.norm, kt, 0:1], bias=lnc[:, n.norm, kt, 1:2])
                ins.then_inc(n.h_hi.sem, 1)
            if 1 in halves:
                L.dense.wait_ready(act, at, uses[1])
                bank = L.dense.bank(at, uses[1])
                for half in range(2):
                    ins = act.activation(r32(hT[64 * half:64 * half + 64, 4, :]), ps[0:64, bank, 0:T], ACT.Identity,
                                         scale=lnc[0:64, n.norm, 2, 0:1], bias=lnc[0:64, n.norm, 2, 1:2])
                ins.then_inc(n.h_hi.sem, 1)

        def ln_whole(dve, L, n, p, at, uses):
            for kt in range(KT):
                rows = min(128, D - 128 * kt)
                if kt != 1:
                    dve.wait_ge(n.h_hi.sem, n.h_hi.at(p, 1 + kt // 2))
                ins = dve.tensor_scalar(L.h[0:rows, kt, :], ps[0:rows, L.dense.bank(at, uses[kt // 2]), (kt % 2) * T:(kt % 2) * T + T],
                                        lnc[0:rows, n.norm, kt, 0:1], lnc[0:rows, n.norm, kt, 1:2], ALU.mult, ALU.add)
                if kt:
                    L.dense.release(ins, at, uses[kt - 1])

        def ln_lo(pool, L, n, at, uses, hT):
            for kt in range(KT):
                rows = min(128, D - 128 * kt)
                if kt != 1:
                    L.dense.wait_used(pool, at, uses[kt // 2])
                ins = pool.tensor_tensor(r32(hT[0:rows, 2 * kt + 1, :]), L.h[0:rows, kt, :], hT[0:rows, 2 * kt, :], ALU.subtract)
            ins.then_inc(n.h_lo.sem, 1)

        def part_first(act, L, p, at, u, use, rows, cols, stored):
            L.dense.wait_ready(act, at, use)
            st = L.stored[u % len(L.stored)]
            act.wait_ge(st.sem, st.at(p, stored))
            act.copy(L.parts[u % len(L.stored)][0:rows, 0, 0:cols], ps[0:rows, L.dense.bank(at, use), 0:cols])\
               .then_inc(L.part0.sem, 1)

        def part_second(act, L, p, at, u, use, rows, cols, stored):
            L.dense.wait_used(act, at, use)
            act.copy(L.parts[u % len(L.stored)][0:rows, 1, 0:cols], L.rest[u % len(L.stored)][0:rows, 0:cols])\
               .then_inc(L.part1.sem, 1)

        def parts_act(act, L, p, at, units):
            for i, unit in enumerate(units):
                part_first(act, L, p, at, *unit)
                if i:
                    part_second(act, L, p, at, *units[i - 1])
            part_second(act, L, p, at, *units[-1])

        def parts_dve(dve, L, p, at, units):
            for u, use, rows, cols, _ in units:
                dve.wait_ge(L.part0.sem, L.part0.at(p, u + 1))
                dve.wait_ge(L.part2.sem, L.part2.at(p, u + 1 - len(L.stored)))
                slot = u % len(L.stored)
                ins = dve.tensor_tensor(L.rest[slot][0:rows, 0:cols], ps[0:rows, L.dense.bank(at, use), 0:cols],
                                        L.parts[slot][0:rows, 0, 0:cols], ALU.subtract)
                L.dense.release(ins, at, use)

        def parts_pool(pool, L, p, units):
            for u, _, rows, cols, _ in units:
                pool.wait_ge(L.part1.sem, L.part1.at(p, u + 1))
                slot = u % len(L.stored)
                pool.tensor_tensor(L.parts[slot][0:rows, 2, 0:cols], L.rest[slot][0:rows, 0:cols],
                                   L.parts[slot][0:rows, 1, 0:cols], ALU.subtract).then_inc(L.part2.sem, 1)

        def store_parts(sp, L, p, u, rows, tiles, cols, dst):
            slot = u % len(L.stored)
            sp.wait_ge(L.part2.sem, L.part2.at(p, u + 1))
            for c in range(3):
                src = L.parts[slot][0:rows, c, 0:tiles * cols]
                if tiles > 1:
                    src = src.rearrange("p (m t) -> p m t", m=tiles)
                    d = dst[c].rearrange("a (m p) t -> p (a m) t", p=128)
                else:
                    d = dst[c].rearrange("a p t -> p (a t)")
                sp.dma_start(d, src).then_inc(L.stored[slot].sem, 16)

        def load_stack(sp, stack, parts, src, sem):
            for g, c in enumerate(parts):
                sp.dma_start(stack[DH * g:DH * g + DH], src[c].rearrange("a (h d) t -> d (a h) t", d=DH)).then_inc(sem, 16)

        def max_dve(dve, L, p, m, heads, b, h0, width):
            dve.wait_ge(L.max_ready.sem, L.max_ready.at(p, m + 1))
            src = ps[0:N, L.max_banks[m % len(L.max_banks)], 0:heads * width]
            if heads > 1:
                src = src.rearrange("p (h j) -> p h j", h=heads)
            dve.tensor_reduce(L.mx[:, b, h0:h0 + heads], src, AX.X, ALU.max).then_inc(L.max_used.sem, 1)

        def negmax_dve(dve, L, p, b, m_done):
            dve.wait_ge(L.max_used.sem, L.max_used.at(p, m_done))
            dve.tensor_scalar(L.nm_hi[:, b, :], L.mx[:, b, :], -1.0, None, ALU.mult).then_inc(L.nm_hi_done.sem, 1)
            dve.wait_ge(L.nm_hi_done.sem, L.nm_hi_done.at(p, b + 1))
            dve.tensor_copy(L.nm[:, b, 0:H], L.nm_hi[:, b, :])
            dve.scalar_tensor_tensor(out=L.nm[:, b, H:2 * H], in0=L.mx[:, b, :], scalar=-1.0, in1=L.nm_hi[:, b, :],
                                     op0=ALU.mult, op1=ALU.subtract).then_inc(L.nm_done.sem, 1)

        def negmax_turn(pe, L, p, at, use, batches):
            pe.wait_ge(L.nm_done.sem, L.nm_done.at(p, batches[-1] + 1))
            L.dense.wait_free(pe, at, use)
            for i, b in enumerate(batches):
                mm = pe.transpose(ps[:, L.dense.bank(at, use), i * N:i * N + N], L.nm[:, b, :], eye[0:N, 0:N])
            mm.then_inc(L.dense.ready.sem, 1)

        def negmax_rows(dve, L, p, at, use, batches):
            L.dense.wait_ready(dve, at, use)
            for b in batches:
                dve.wait_ge(L.nmrow_loaded[b].sem, L.nmrow_loaded[b].at(p, 0))
            src = ps[0:2 * H, L.dense.bank(at, use), 0:len(batches) * N].rearrange("p (b t) -> p b t", t=N)
            ins = dve.tensor_copy(L.nmrow[:, batches[0]:batches[-1] + 1, :], src)
            L.dense.release(ins, at, use)

        def negmax_send(sp, L, at, use, batches):
            L.dense.wait_used(sp, at, use)
            for b in batches:
                for i in range(2):
                    sp.dma_start(L.qs[STACK + i:STACK + i + 1, :, b * N:b * N + N], L.nmrow[i * H:i * H + H, b, :])\
                      .then_inc(L.nmrow_loaded[b].sem, 16)

        def scores_pe(pe, L, p, i, ks, tiles, keys, keys_at):
            g, jt = divmod(i, tiles)
            b, hg = divmod(g, HG)
            if hg == 0 and jt == 0:
                pe.wait_ge(L.nmrow_loaded[b].sem, L.nmrow_loaded[b].at(p, 32))
            pe.wait_ge(L.exp_done.sem, L.exp_done.at(p, i + 1 - len(L.st_banks)))
            for hh in range(4):
                k0 = keys_at + jt * keys
                mm = pe.matmul(ps[0:keys, L.st_banks[i % len(L.st_banks)], hh * N:hh * N + N], ks[0:STACK + 2, 4 * hg + hh, k0:k0 + keys],
                               L.qs[0:STACK + 2, 4 * hg + hh, b * N:b * N + N], start=True, stop=True)
            mm.then_inc(L.st_ready.sem, 1)

        def exp_act(act, L, p, g, tiles, keys):
            act.wait_ge(L.pv_done.sem, L.pv_done.at(p, g - 1))
            for jt in range(tiles):
                i = g * tiles + jt
                act.wait_ge(L.st_ready.sem, L.st_ready.at(p, i + 1))
                act.activation(L.probs[0:keys, i % (2 * tiles), :], ps[0:keys, L.st_banks[i % len(L.st_banks)], 0:4 * N], ACT.Exp,
                               scale=SCALE).then_inc(L.exp_done.sem, 1)

        def values_pe(pe, L, p, i, values, tiles, keys):
            g, jt = divmod(i, tiles)
            if jt == 0:
                pe.wait_ge(L.ot_done.sem, L.ot_done.at(p, g + 1 - len(L.pv_banks)))
            pe.wait_ge(L.exp_done.sem, L.exp_done.at(p, i + 1))
            for hh in range(4):
                h = 4 * (g % HG) + hh
                mm = pe.matmul(ps[32 * hh:32 * hh + VW, L.pv_banks[g % len(L.pv_banks)], 0:N], values[0:keys, jt, h * VW:(h + 1) * VW],
                               L.probs[0:keys, i % (2 * tiles), hh * N:hh * N + N], start=jt == 0, stop=jt == tiles - 1)
            if jt == tiles - 1:
                mm.then_inc(L.pv_done.sem, 1)

        def values_act(act, L, p, g):
            b, hg = divmod(g, HG)
            act.wait_ge(L.pv_done.sem, L.pv_done.at(p, g + 1))
            act.copy(L.ot[:, b, hg * N:hg * N + N], ps[:, L.pv_banks[g % len(L.pv_banks)], 0:N]).then_inc(L.ot_done.sem, 1)

        def tail_turn(pe, L, p, b, at):
            pe.wait_ge(L.ot_done.sem, L.ot_done.at(p, HG * (b + 1)))
            for use, groups in ((f"t{b}a", range(4)), (f"t{b}b", range(4, HG))):
                L.dense.wait_free(pe, at, use)
                for i, hg in enumerate(groups):
                    mm = pe.transpose(ps[0:N, L.dense.bank(at, use), 128 * i:128 * i + 128], L.ot[:, b, hg * N:hg * N + N], eye[:, :])
                mm.then_inc(L.dense.ready.sem, 1)

        def tail_divide(dve, L, p, b, at):
            for half, (use, h0, heads) in enumerate([(f"t{b}a", 0, 16), (f"t{b}b", 16, 4)]):
                L.dense.wait_ready(dve, at, use)
                src = ps[0:N, L.dense.bank(at, use), 0:heads * 32].rearrange("p (h c) -> p h c", c=32)
                dve.reciprocal(L.rsum[:, h0:h0 + heads], src[:, :, DH]).then_inc(L.rsum_done.sem, 1)
                dve.wait_ge(L.rsum_done.sem, L.rsum_done.at(p, 2 * b + half + 1))
                ins = dve.tensor_tensor(L.on[:, h0 * DH:(h0 + heads) * DH].rearrange("p (h d) -> p h d", d=DH), src[:, :, 0:DH],
                                        L.rsum[:, h0:h0 + heads].unsqueeze(2).broadcast_to([N, heads, DH]), ALU.mult)
                L.dense.release(ins, at, use)

        def tail_return(pe, L, b, at):
            use = f"t{b}c"
            L.dense.wait_free(pe, at, use)
            L.dense.wait_used(pe, at, f"t{b}b")
            for kt in range(KT):
                rows = min(128, D - 128 * kt)
                mm = pe.transpose(ps[0:rows, L.dense.bank(at, use), kt * N:kt * N + N], L.on[:, 128 * kt:128 * kt + rows], eye[0:N, 0:N])
            mm.then_inc(L.dense.ready.sem, 1)

        def tail_hi(act, L, p, b, at):
            L.dense.wait_ready(act, at, f"t{b}c")
            bank = L.dense.bank(at, f"t{b}c")
            act.copy(r32(L.onT[:, 0:3:2, :]), ps[:, bank, 0:2 * N].rearrange("p (k t) -> p k t", k=2))
            for half in range(2):
                ins = act.copy(r32(L.onT[64 * half:64 * half + 64, 4, :]), ps[0:64, bank, 2 * N:3 * N])
            ins.then_inc(L.on_hi.sem, 1)

        def tail_lo(dve, L, p, b, at):
            dve.wait_ge(L.on_hi.sem, L.on_hi.at(p, b + 1))
            bank = L.dense.bank(at, f"t{b}c")
            dve.tensor_tensor(r32(L.onT[:, 1:4:2, :]), ps[:, bank, 0:2 * N].rearrange("p (k t) -> p k t", k=2),
                              L.onT[:, 0:3:2, :], ALU.subtract)
            ins = dve.tensor_tensor(r32(L.onT[0:64, 5, :]), ps[0:64, bank, 2 * N:3 * N], L.onT[0:64, 4, :], ALU.subtract)
            L.dense.release(ins, at, f"t{b}c")

        def tail_product(pe, L, b, at, w, w0):
            L.dense.wait_used(pe, at, f"t{b}c")
            rows_product(pe, L, at, f"o{b}", L.onT, 0, N, w, w0, PASSES_D)

        def tail_add(dve, L, p, b, at):
            L.dense.wait_ready(dve, at, f"o{b}")
            dve.wait_ge(L.xb_done.sem, L.xb_done.at(p, 1))
            ins = dve.tensor_tensor(L.xo[:, b], ps[0:N, L.dense.bank(at, f"o{b}"), 0:D], L.xb[:, b], ALU.add)
            L.dense.release(ins, at, f"o{b}")

        def rows_product(pe, L, at, use, xT, c0, tokens, w, w0, passes):
            L.dense.wait_free(pe, at, use)
            for i, (xs, ws, rows) in enumerate(passes):
                mm = pe.matmul(ps[0:tokens, L.dense.bank(at, use), 0:D], r32(xT[0:rows, xs, c0:c0 + tokens]),
                               r32(w[0:rows, ws, w0:w0 + D]), start=i == 0, stop=i == len(passes) - 1)
            mm.then_inc(L.dense.ready.sem, 1)

        def cols_product(pe, L, at, use, xT, w, blocks, passes):
            L.dense.wait_free(pe, at, use)
            width = xT.shape[2]
            for j, (w0, m) in enumerate(blocks):
                for i, (xs, ws, rows) in enumerate(passes):
                    mm = pe.matmul(ps[0:m, L.dense.bank(at, use), j * width:j * width + width], r32(w[0:rows, ws, w0:w0 + m]),
                                   r32(xT[0:rows, xs, :]), start=i == 0, stop=i == len(passes) - 1)
            mm.then_inc(L.dense.ready.sem, 1)

        def common(ctx, tag, dense_parts, parts_per, slots, slot_stores, maxima, banks, tiles, part_cols):
            L = Loop()
            L.signals = []

            def sig(name, per, lead=1):
                s = Signal(ctx, nc, f"{tag}_{name}", per, lead)
                L.signals.append(s)
                return s

            def norm(number, calls):
                n = Norm()
                n.norm = number
                name = f"ln{number}_"
                n.stats_done = sig(name + "stats_done", calls)
                n.aggr_done = sig(name + "aggr_done", calls)
                n.var_done = sig(name + "var_done", calls)
                n.rstd_done = sig(name + "rstd_done", calls)
                n.z_done = sig(name + "z_done", calls)
                n.h_hi = sig(name + "h_hi", 2)
                n.h_lo = sig(name + "h_lo", 1)
                n.stats = sbt(ctx, tag + name + "stats", [N, 2, 6])
                n.mv = sbt(ctx, tag + name + "mv", [N, 2, 2])
                n.ve = sbt(ctx, tag + name + "ve", [N, 2])
                n.rstd = sbt(ctx, tag + name + "rstd", [N, 2])
                return n

            L.sig, L.norm = sig, norm
            L.st_banks, L.max_banks, L.pv_banks, dense_banks = banks
            L.dense = Ring(ctx, nc, tag + "_dense", dense_banks, dense_parts)
            L.signals += [L.dense.ready, *L.dense.used]
            L.part0 = sig("part0", parts_per)
            L.part1 = sig("part1", parts_per)
            L.part2 = sig("part2", parts_per, slots)
            L.stored = [Signal(ctx, nc, f"{tag}_stored{i}", slot_stores) for i in range(slots)]
            L.signals += L.stored
            L.max_ready = sig("max_ready", maxima)
            L.max_used = sig("max_used", maxima, 4)
            L.nm_hi_done = sig("nm_hi_done", 2)
            L.nm_done = sig("nm_done", 2)
            L.on_hi = sig("on_hi", 2)
            L.rsum_done = sig("rsum_done", 4)
            L.nmrow_loaded = [sig(f"nmrow_loaded{b}", 32) for b in range(2)]
            L.st_ready = sig("st_ready", 2 * HG * tiles)
            L.exp_done = sig("exp_done", 2 * HG * tiles, 3)
            L.pv_done = sig("pv_done", 2 * HG, 2)
            L.ot_done = sig("ot_done", 2 * HG, 2)
            L.x_loaded = sig("x_loaded", 16)
            L.xb_loaded = sig("xb_loaded", 16)
            L.xb_done = sig("xb_done", 1)
            L.tick = sbt(ctx, tag + "_tick", [1, 2])
            L.x = sbt(ctx, tag + "_x", [N, 2, D])
            L.xb = sbt(ctx, tag + "_xb", [N, 2, D])
            L.xo = sbt(ctx, tag + "_xo", [N, 2, D])
            L.z = sbt(ctx, tag + "_z", [N, 2, 128 * KT])
            L.h = sbt(ctx, tag + "_h", [128, KT, T])
            L.hT = sbt(ctx, tag + "_hT", [128, 6, T])
            L.parts = [sbt(ctx, f"{tag}_parts{i}", [128, 3, part_cols], BF16) for i in range(slots)]
            L.rest = [sbt(ctx, f"{tag}_rest{i}", [128, part_cols]) for i in range(slots)]
            L.qs = sbt(ctx, tag + "_qs", [STACK + 2, H, T], BF16)
            L.mx = sbt(ctx, tag + "_mx", [N, 2, H])
            L.nm_hi = sbt(ctx, tag + "_nm_hi", [N, 2, H], BF16)
            L.nm = sbt(ctx, tag + "_nm", [N, 2, 128])
            L.nmrow = sbt(ctx, tag + "_nmrow", [2 * H, 2, N], BF16)
            L.probs = sbt(ctx, tag + "_probs", [128, 2 * tiles, 4 * N])
            L.ot = sbt(ctx, tag + "_ot", [128, 2, HG * N])
            L.rsum = sbt(ctx, tag + "_rsum", [N, H])
            L.on = sbt(ctx, tag + "_on", [N, D])
            L.onT = sbt(ctx, tag + "_onT", [128, 6, N])
            return L

        def begin(eng, L):
            for s in L.signals:
                eng.sem_inc(s.sem, s.lead)
            eng.memset(ps[:, L.pv_banks[0]:L.pv_banks[-1] + 1, 0:N], 0.0)
            eng.memset(L.z[:], 0.0)
            eng.memset(L.nm[:], 0.0)

        def load_x(sp, L, n, before, src):
            if before is not None:
                sp.wait_ge(n.z_done.sem, n.z_done.at(before, 1))
            sp.dma_start(L.x[:], src.rearrange("b n d -> n b d")).then_inc(L.x_loaded.sem, 16)

        def load_xb(sp, L, src):
            sp.dma_start(L.xb[:], src.rearrange("b n d -> n b d")).then_inc(L.xb_loaded.sem, 16)

        def bias_add(pool, L, p, row):
            pool.wait_ge(L.xb_loaded.sem, L.xb_loaded.at(p, 16))
            pool.tensor_tensor(L.xb[:], L.xb[:], brow[:, row:row + 1, :].broadcast_to([N, 2, D]), ALU.add).then_inc(L.xb_done.sem, 1)

        def overlay(name, names):
            with ExitStack() as ctx:
                return [sbt(ctx, f"{name}{i}", [128, 3, 2 * D]) for i in names]

        wqo = sbt(top, "wqo", [128, 5, 2 * D])
        raw_first = overlay("raw_first", (0, 1))
        wf1 = sbt(top, "wf1", [128, 5, 2 * F])
        wf2 = sbt(top, "wf2", [128, FT, 2, D])

        with ExitStack() as ctx:
            CONTEXT = [[f"c{b}{kind}{m}" for kind in "kv" for m in range(3)] for b in range(2)]
            BODY = ["h0", "h1", "c1k2", "c1v0", "c1v1", "c1v2", "qk0", "qk1", "qk2", "c0k0", "nm", "c0k1", "c0k2", "c0v0",
                    "c0v1", "c0v2", "t0a", "t0b", "v0", "t0c", "o0", "t1a", "t1b", "v1", "c1k0", "t1c", "c1k1", "o1"]
            STAGE = ["h0", "h1", "qk0", "qk1", "qk2", "v0", "v1"] + CONTEXT[0] + CONTEXT[1][0:2]
            L = common(ctx, "a", [("pro", STAGE, 0, 1), ("loop", BODY, 0, PAIRS - 2),
                                  ("late", BODY, PAIRS - 2, 1), ("last", [n for n in BODY if n not in STAGE], PAIRS - 1, 1)],
                       9, 3, 16 * 9, 2 * HG, ((0, 1), (2, 3, 0, 1), (2, 3), (4, 5, 6, 7)), 1, 2 * T)
            ln1 = L.norm(0, 1)
            raw_rest = overlay("raw_rest", (0,))
            wqk = sbt(ctx, "wqk", [128, 5, 2 * D])
            raw_rest += overlay("raw_rest", (1,))
            wkv = sbt(ctx, "wkv", [128, 3, 2 * D])
            wvo = sbt(ctx, "wvo", [128, 5, 2 * D])
            chunks = [("d", [(q1, 0, D), (k1, D, D)], wqk, 0, 2 * D),
                      ("d", [(v1, 0, D), (o1, D, D)], wvo, 0, 2 * D),
                      ("c", [(k2, 0, D), (v2, D, D)], wkv, 0, 2 * D),
                      ("d", [(q2, 0, D), (o2, D, D)], wqo, 0, 2 * D)]
            chunks += [("d", [(w1[:, c:c + 2 * D], 0, 2 * D)], wf1, c, 2 * D) for c in range(0, 2 * F, 2 * D)]
            chunks += [("f", [(w2, 0, D)], wf2, 0, 6), ("f", [(w2, 0, D)], wf2, 6, FT - 6)]
            FIRST, REST = range(3), range(3, len(chunks))
            W = Weights()
            W.raw = [(raw_first if i in FIRST else raw_rest)[(i - 3) % 2] for i in range(len(chunks))]
            W.loaded = [Signal(ctx, nc, f"w_loaded{i}", 0, 0) for i in range(len(chunks))]
            W.hi = Signal(ctx, nc, "w_hi", 0, 0)
            W.lo = Signal(ctx, nc, "w_lo", 0, 0)

            ks = sbt(ctx, "a_ks", [STACK + 2, H, T], BF16)
            ctxr = sbt(ctx, "ctxr", [128, 2, JP])
            ctxT = sbt(ctx, "ctxT", [128, 4, JP])
            va = sbt(ctx, "va", [N, 2, H * VW])
            vc = sbt(ctx, "vc", [JW, 2, JT, H * VW])
            init_done = Signal(ctx, nc, "init_done", 0, 0)
            ks_ones = Signal(ctx, nc, "ks_ones", 0, 0)
            ctx_loaded = L.sig("ctx_loaded", 96)
            ctx_hi = L.sig("ctx_hi", 2)
            ctx_lo = L.sig("ctx_lo", 2)
            stack_loaded = L.sig("stack_loaded", 16 * 12)
            vc_stored = [L.sig(f"vc_stored{b}", 16) for b in range(2)]
            xo_stored = L.sig("xo_stored", 16)

            units_qk = [(u, f"qk{u}", 128, 2 * T if u < 2 else T, 0) for u in range(3)]
            units_k2 = [[(3 + 3 * b + m, f"c{b}k{m}", min(128, D - 128 * m), JP, 48 * (b + 1)) for m in range(KT)]
                        for b in range(2)]

            with nc.Block() as block:
                @block.sync
                def _(sp):
                    load_x(sp, L, ln1, None, x[0:2])
                    for dst, src in ((eye, ident), (lnc, ln_cols), (b1c, b1_cols), (brow, bias_rows)):
                        d = dst[:]
                        if len(dst.shape) > 2:
                            d = d.rearrange("p a b c -> p (a b c)" if len(dst.shape) == 4 else "p a b -> p (a b)")
                        sp.dma_start(d, src).then_inc(const_loaded.sem, 16)

                    def load_ctx(c):
                        for dst, lo, hi in ((ctxr[:, 0, 0:J], 0, 128), (ctxr[0:64, 1, 0:J], 128, CTX), (ctxr[64:128, 1, 0:J], 128, CTX)):
                            sp.dma_start(dst, c[:, lo:hi].rearrange("a c t -> c (a t)")).then_inc(ctx_loaded.sem, 16)

                    def store_qk(s, row, units):
                        for u, tiles, r0 in [((0, 2, 0), (1, 2, 256), (2, 1, 512))[u] for u in units]:
                            store_parts(sp, L, s, u, 128, tiles, T,
                                        [qk_scr[bass.ds(row, 1), c, r0:r0 + 128 * tiles] for c in range(3)])

                    def wait_stored(s, count):
                        for st in L.stored:
                            sp.wait_ge(st.sem, st.at(s, count))

                    def load_stacks(row):
                        load_stack(sp, L.qs, Q_PARTS, [qk_scr[bass.ds(row, 1), c, 0:D] for c in range(3)], stack_loaded.sem)
                        load_stack(sp, ks, K_PARTS, [qk_scr[bass.ds(row, 1), c, D:2 * D] for c in range(3)], stack_loaded.sem)

                    load_weights(sp, W, chunks, FIRST)
                    sp.wait_ge(init_done.sem, 1)
                    load_ctx(ctx_t[0:1])
                    load_x(sp, L, ln1, 0, x[2:4])
                    load_xb(sp, L, x[0:2])
                    sp.wait_ge(ctx_lo.sem, ctx_lo.at(0, 1))
                    load_ctx(ctx_t[1:2])

                    def store_keys(s, b, tiles, row):
                        for m in tiles:
                            store_parts(sp, L, s, 3 + 3 * b + m, min(128, D - 128 * m), 1, JP,
                                        [k2_scr[bass.ds(row, 1), c, 128 * m:min(D, 128 * m + 128)] for c in range(3)])

                    def store_values(at, b, row):
                        L.dense.wait_used(sp, at, f"c{b}v2")
                        sp.dma_start(v2_scr[bass.ds(row, 1)].rearrange("a p c -> p (a c)"),
                                     vc[:, b].rearrange("p t c -> p (t c)")).then_inc(vc_stored[b].sem, 16)

                    store_qk(0, 0, range(3))
                    wait_stored(0, 48)
                    load_stacks(0)
                    store_keys(0, 0, range(3), 0)
                    store_values(("pro", 0), 0, 0)
                    store_keys(0, 1, range(2), 1)

                    def body(p, at):
                        stage = at[0] != "last"
                        if stage:
                            sp.wait_ge(ctx_lo.sem, ctx_lo.at(p, 2))
                            load_ctx(ctx_t[bass.ds(2 * p + 2, 1)])
                        else:
                            load_weights(sp, W, chunks, REST[:1])
                        store_keys(p, 1, range(2, 3), 2 * p + 1)
                        store_values(at, 1, 2 * p + 1)
                        if at[0] == "loop":
                            load_x(sp, L, ln1, (p, 1), x[bass.ds(2 * p + 4, 2)])
                        if not stage:
                            load_weights(sp, W, chunks, REST[1:3])
                        if stage:
                            sp.wait_ge(ctx_lo.sem, ctx_lo.at((p, 1), 1))
                            load_ctx(ctx_t[bass.ds(2 * p + 3, 1)])
                            store_qk((p, 1), p + 1, range(2))
                        negmax_send(sp, L, at, "nm", range(2))
                        if stage:
                            store_qk((p, 1), p + 1, range(2, 3))
                            store_keys((p, 1), 0, range(3), 2 * p + 2)
                            store_values(at, 0, 2 * p + 2)
                            sp.wait_ge(L.st_ready.sem, L.st_ready.at(p, 2 * HG))
                            wait_stored((p, 1), 96)
                            load_stacks(p + 1)
                            store_keys((p, 1), 1, range(2), 2 * p + 3)
                        L.dense.wait_used(sp, at, "o1")
                        sp.dma_start(x1_scr[bass.ds(2 * p, 2)].rearrange("b n d -> n b d"), L.xo[:]).then_inc(xo_stored.sem, 16)
                        if stage:
                            load_xb(sp, L, x[bass.ds(2 * p + 2, 2)])
                        else:
                            load_weights(sp, W, chunks, REST[3:])

                    with sp.Fori(0, PAIRS - 2) as p:
                        body(p, ("loop", p))
                    body(PAIRS - 2, ("late", PAIRS - 2))
                    body(PAIRS - 1, ("last", PAIRS - 1))
                    for s in [*L.stored, *vc_stored, xo_stored]:
                        sp.wait_ge(s.sem, s.at(PAIRS, 0))

                @block.tensor
                def _(pe):
                    def stage_norm(s, at):
                        ln_turn(pe, L, ln1, s, at, ("h0", "h1"))

                    def stage_qk(s, at, i):
                        if i == 0:
                            pe.wait_ge(ln1.h_lo.sem, ln1.h_lo.at(s, 1))
                        blocks = ([(0, 128), (128, 128)], [(256, 128), (384, 128)], [(512, 128)])[i]
                        cols_product(pe, L, at, f"qk{i}", L.hT, wqk, blocks, PASSES_D)

                    def stage_v(at, b):
                        rows_product(pe, L, at, f"v{b}", L.hT, b * N, N, wvo, 0, PASSES_D)

                    def context(p, at, b, i):
                        if i == 0:
                            pe.wait_ge(ctx_lo.sem, ctx_lo.at(p, b + 1))
                        if i < KT:
                            cols_product(pe, L, at, CONTEXT[b][i], ctxT, wkv, [(128 * i, min(128, D - 128 * i))], PASSES_C)
                        else:
                            rows_product(pe, L, at, CONTEXT[b][i], ctxT, (i - KT) * JW, JW, wkv, D, PASSES_C)

                    def group_max(p, g):
                        b, hg = divmod(g, HG)
                        pe.wait_ge(L.max_used.sem, L.max_used.at(p, g - len(L.max_banks) + 1))
                        for hh in range(4):
                            t = slice(b * N, b * N + N)
                            mm = pe.matmul(ps[0:N, L.max_banks[g % len(L.max_banks)], hh * N:hh * N + N], L.qs[0:STACK, 4 * hg + hh, t],
                                           ks[0:STACK, 4 * hg + hh, t], start=True, stop=True)
                        mm.then_inc(L.max_ready.sem, 1)

                    pe.wait_ge(const_loaded.sem, 64)
                    pe.wait_ge(init_done.sem, 1)
                    pe.wait_ge(W.lo.sem, 1)
                    stage_norm(0, ("pro", 0))
                    for i in range(3):
                        stage_qk(0, ("pro", 0), i)
                    pe.wait_ge(W.lo.sem, 2)
                    for b in range(2):
                        stage_v(("pro", 0), b)
                    pe.wait_ge(W.lo.sem, 3)
                    for i in range(6):
                        context(0, ("pro", 0), 0, i)
                    for i in range(2):
                        context(0, ("pro", 0), 1, i)
                    pe.wait_ge(ks_ones.sem, 1)

                    def body(p, at):
                        stage = at[0] != "last"
                        if stage:
                            stage_norm((p, 1), at)
                        for i in range(2, 6):
                            context(p, at, 1, i)
                        pe.wait_ge(stack_loaded.sem, stack_loaded.at(p, stack_loaded.per))
                        for g in range(2 * HG):
                            group_max(p, g)
                            if stage and g in (3, 5, 7):
                                stage_qk((p, 1), at, (g - 3) // 2)
                        if stage:
                            context((p, 1), at, 0, 0)
                        negmax_turn(pe, L, p, at, "nm", range(2))
                        if stage:
                            for i in range(1, 3):
                                context((p, 1), at, 0, i)
                        for g in range(2 * HG):
                            scores_pe(pe, L, p, g, ks, 1, N, (g // HG) * N)
                            if 2 <= g <= 4 and stage:
                                context((p, 1), at, 0, g + 1)
                            if g == HG + 1:
                                tail_turn(pe, L, p, 0, at)
                                if stage:
                                    stage_v(at, 0)
                            if g == HG + 2:
                                tail_return(pe, L, 0, at)
                            if g == HG + 3:
                                tail_product(pe, L, 0, at, wvo, D)
                            if g:
                                values_pe(pe, L, p, g - 1, va[:, (g - 1) // HG:(g - 1) // HG + 1], 1, N)
                        values_pe(pe, L, p, 2 * HG - 1, va[:, 1:2], 1, N)
                        tail_turn(pe, L, p, 1, at)
                        if stage:
                            stage_v(at, 1)
                            context((p, 1), at, 1, 0)
                        tail_return(pe, L, 1, at)
                        if stage:
                            context((p, 1), at, 1, 1)
                        tail_product(pe, L, 1, at, wvo, D)

                    with pe.Fori(0, PAIRS - 2) as p:
                        body(p, ("loop", p))
                    body(PAIRS - 2, ("late", PAIRS - 2))
                    body(PAIRS - 1, ("last", PAIRS - 1))

                @block.scalar
                def _(act):
                    def context_hi(p, b):
                        act.wait_ge(ctx_loaded.sem, ctx_loaded.at(p, 48 * (b + 1)))
                        act.copy(r32(ctxT[:, 0:3:2, :]), ctxr[:, :, :]).then_inc(ctx_hi.sem, 1)

                    def context_values(p, at, b, tiles):
                        act.wait_ge(vc_stored[b].sem, vc_stored[b].at(p, 0))
                        for jt in tiles:
                            L.dense.wait_ready(act, at, f"c{b}v{jt}")
                            ins = act.copy(vc[:, b, jt].rearrange("p (h c) -> p h c", c=VW)[:, :, 0:DH],
                                           ps[0:JW, L.dense.bank(at, f"c{b}v{jt}"), 0:D].rearrange("p (h d) -> p h d", d=DH))
                            L.dense.release(ins, at, f"c{b}v{jt}")

                    def stage_values(at, b):
                        L.dense.wait_ready(act, at, f"v{b}")
                        ins = act.copy(va[:, b].rearrange("p (h c) -> p h c", c=VW)[:, :, 0:DH],
                                       ps[0:N, L.dense.bank(at, f"v{b}"), 0:D].rearrange("p (h d) -> p h d", d=DH))
                        L.dense.release(ins, at, f"v{b}")

                    act.wait_ge(const_loaded.sem, 64)
                    act.wait_ge(init_done.sem, 1)
                    split_hi(act, W, chunks, range(1))
                    ln_hi(act, L, ln1, ("pro", 0), ("h0", "h1"), L.hT)
                    split_hi(act, W, chunks, range(1, 3))
                    context_hi(0, 0)
                    parts_act(act, L, 0, ("pro", 0), units_qk)
                    for b in range(2):
                        stage_values(("pro", 0), b)
                    parts_act(act, L, 0, ("pro", 0), units_k2[0])
                    context_values(0, ("pro", 0), 0, range(JT))
                    context_hi(0, 1)
                    parts_act(act, L, 0, ("pro", 0), units_k2[1][:2])

                    def body(p, at):
                        stage = at[0] != "last"
                        if stage:
                            ln_hi(act, L, ln1, at, ("h0", "h1"), L.hT)
                        parts_act(act, L, p, at, units_k2[1][2:])
                        context_values(p, at, 1, range(JT))
                        if stage:
                            context_hi((p, 1), 0)
                            parts_act(act, L, (p, 1), at, units_qk)
                        else:
                            split_hi(act, W, chunks, REST[:3])
                        for g in range(2 * HG):
                            exp_act(act, L, p, g, 1, N)
                            if stage:
                                if 1 <= g <= 3:
                                    part_second(act, L, (p, 1), at, *units_k2[0][g - 1])
                                if g <= 2:
                                    part_first(act, L, (p, 1), at, *units_k2[0][g])
                                if 3 <= g <= 5:
                                    context_values((p, 1), at, 0, range(g - 3, g - 2))
                                if g == HG:
                                    context_hi((p, 1), 1)
                                if g == HG + 1:
                                    stage_values(at, 0)
                            if g == HG + 2:
                                tail_hi(act, L, p, 0, at)
                            if g:
                                values_act(act, L, p, g - 1)
                        values_act(act, L, p, 2 * HG - 1)
                        if stage:
                            stage_values(at, 1)
                            part_first(act, L, (p, 1), at, *units_k2[1][0])
                        tail_hi(act, L, p, 1, at)
                        if stage:
                            part_second(act, L, (p, 1), at, *units_k2[1][0])
                            parts_act(act, L, (p, 1), at, units_k2[1][1:2])

                    with act.Fori(0, PAIRS - 2) as p:
                        body(p, ("loop", p))
                    body(PAIRS - 2, ("late", PAIRS - 2))
                    body(PAIRS - 1, ("last", PAIRS - 1))
                    split_hi(act, W, chunks, REST[3:])

                @block.vector
                def _(dve):
                    begin(dve, L)
                    dve.wait_ge(const_loaded.sem, 64)
                    dve.wait_ge(init_done.sem, 1)
                    dve.wait_ge(L.x_loaded.sem, L.x_loaded.at(0, 16))
                    ln_stats(dve, L, ln1, 0, 0, L.x, range(2))
                    ln_scale(dve, L, ln1, 0, 0, L.x, range(2))
                    split_lo(dve, W, chunks, range(1))
                    ln_whole(dve, L, ln1, 0, ("pro", 0), ("h0", "h1"))
                    split_lo(dve, W, chunks, range(1, 3))
                    parts_dve(dve, L, 0, ("pro", 0), units_qk)
                    dve.memset(ks[STACK:STACK + 2], 1.0).then_inc(ks_ones.sem, 1)
                    dve.wait_ge(L.x_loaded.sem, L.x_loaded.at(1, 16))
                    ln_stats(dve, L, ln1, 1, 0, L.x, range(2))
                    parts_dve(dve, L, 0, ("pro", 0), units_k2[0])
                    ln_scale(dve, L, ln1, 1, 0, L.x, range(2))
                    parts_dve(dve, L, 0, ("pro", 0), units_k2[1][:2])

                    def body(p, at):
                        stage, far = at[0] != "last", at[0] == "loop"
                        if stage:
                            ln_whole(dve, L, ln1, (p, 1), at, ("h0", "h1"))
                        parts_dve(dve, L, p, at, units_k2[1][2:])
                        for g in range(2 * HG):
                            max_dve(dve, L, p, g, 4, g // HG, 4 * (g % HG), N)
                            if g % HG == HG - 1:
                                negmax_dve(dve, L, p, g // HG, g + 1)
                            if stage and g in (5, 7):
                                parts_dve(dve, L, (p, 1), at, [units_qk[(g - 5) // 2]])
                        negmax_rows(dve, L, p, at, "nm", range(2))
                        if stage:
                            parts_dve(dve, L, (p, 1), at, units_qk[2:])
                            parts_dve(dve, L, (p, 1), at, units_k2[0])
                        else:
                            split_lo(dve, W, chunks, REST[:3])
                        if far:
                            dve.wait_ge(L.x_loaded.sem, L.x_loaded.at((p, 2), 16))
                            ln_stats(dve, L, ln1, (p, 2), 0, L.x, range(2))
                        dve.wait_ge(xo_stored.sem, xo_stored.at(p, 0))
                        tail_divide(dve, L, p, 0, at)
                        if far:
                            ln_scale(dve, L, ln1, (p, 2), 0, L.x, range(2))
                        tail_lo(dve, L, p, 0, at)
                        tail_add(dve, L, p, 0, at)
                        tail_divide(dve, L, p, 1, at)
                        if stage:
                            parts_dve(dve, L, (p, 1), at, units_k2[1][:1])
                        tail_lo(dve, L, p, 1, at)
                        if stage:
                            parts_dve(dve, L, (p, 1), at, units_k2[1][1:2])
                        tail_add(dve, L, p, 1, at)

                    with dve.Fori(0, PAIRS - 2) as p:
                        body(p, ("loop", p))
                    body(PAIRS - 2, ("late", PAIRS - 2))
                    body(PAIRS - 1, ("last", PAIRS - 1))
                    split_lo(dve, W, chunks, REST[3:])

                @block.gpsimd
                def _(pool):
                    pool.memset(neghalf[:], -0.5)
                    pool.memset(epsc[:], EPS)
                    pool.memset(ctxr[:], 0.0)
                    pool.memset(va[:], 1.0)
                    pool.memset(vc[:], 1.0).then_inc(init_done.sem, 1)
                    pool.wait_ge(const_loaded.sem, 64)

                    def context_lo(p, b):
                        pool.wait_ge(ctx_hi.sem, ctx_hi.at(p, b + 1))
                        pool.tensor_tensor(r32(ctxT[:, 1, :]), ctxr[:, 0, :], ctxT[:, 0, :], ALU.subtract)
                        pool.tensor_tensor(r32(ctxT[0:64, 3, :]), ctxr[0:64, 1, :], ctxT[0:64, 2, :], ALU.subtract)\
                            .then_inc(ctx_lo.sem, 1)

                    ln_rstd(pool, ln1, 0, 0, range(2))
                    ln_lo(pool, L, ln1, ("pro", 0), ("h0", "h1"), L.hT)
                    context_lo(0, 0)
                    parts_pool(pool, L, 0, units_qk)
                    ln_rstd(pool, ln1, 1, 0, range(2))
                    parts_pool(pool, L, 0, units_k2[0])
                    context_lo(0, 1)
                    parts_pool(pool, L, 0, units_k2[1][:2])

                    def body(p, at):
                        stage = at[0] != "last"
                        if stage:
                            ln_lo(pool, L, ln1, at, ("h0", "h1"), L.hT)
                        parts_pool(pool, L, p, units_k2[1][2:])
                        if stage:
                            context_lo((p, 1), 0)
                            parts_pool(pool, L, (p, 1), units_qk)
                        bias_add(pool, L, p, 0)
                        if stage:
                            parts_pool(pool, L, (p, 1), units_k2[0])
                            if at[0] == "loop":
                                ln_rstd(pool, ln1, (p, 2), 0, range(2))
                            context_lo((p, 1), 1)
                            parts_pool(pool, L, (p, 1), units_k2[1][:2])

                    with pool.Fori(0, PAIRS - 2) as p:
                        body(p, ("loop", p))
                    body(PAIRS - 2, ("late", PAIRS - 2))
                    body(PAIRS - 1, ("last", PAIRS - 1))

        with ExitStack() as ctx:
            BODY = ["f0", "f1", "f2", "f3", "nm0", "f4", "f5", "f6", "nm1", "f7", "h0", "h1", "t0a", "t0b", "q0", "t0c", "q1",
                    "o0", "f8", "t1a", "t1b", "t1c", "o1", "f9", "g0", "g1"]
            STAGE = ["h0", "h1", "q0", "q1"]
            FEED = [f"f{i}" for i in range(FT)]
            L = common(ctx, "c", [("pro", STAGE, 0, 1), ("first", [n for n in BODY if n not in FEED], 0, 1),
                                  ("loop", BODY, 1, PAIRS - 2), ("last", [n for n in BODY if n not in STAGE], PAIRS - 1, 1),
                                  ("epi", FEED, PAIRS, 1)],
                       2, 2, 48, 2 * H, ((0, 1, 4), (5, 0, 1, 4), (5,), (6, 7)), JT, 2 * T)
            ln2, ln3 = L.norm(1, 1), L.norm(2, 2)
            BK_ACC = 2
            h3T = sbt(ctx, "h3T", [128, 6, T])
            x3b = sbt(ctx, "x3b", [N, 2, D])
            gl = sbt(ctx, "gl", [128, 2, T])
            uf = sbt(ctx, "uf", [128, 2, T])
            UR = 5
            uT = sbt(ctx, "uT", [128, UR, 2, T])
            kc = [sbt(ctx, f"kc{b}", [STACK + 2, H, JP], BF16) for b in range(2)]
            vc = [sbt(ctx, f"vcc{b}", [JW, JT, H * VW]) for b in range(2)]
            ones_done = Signal(ctx, nc, "ones_done", 0, 0)
            x3b_done = L.sig("x3b_done", 1)
            k_loaded = [L.sig(f"k_loaded{b}", 96) for b in range(2)]
            v_loaded = [L.sig(f"v_loaded{b}", 16) for b in range(2)]
            q_loaded = L.sig("q_loaded", 96)
            out_stored = L.sig("out_stored", 16)
            gelu_done = L.sig("gelu_done", FT)
            u_hi = L.sig("u_hi", FT)
            u_lo = L.sig("u_lo", FT, 2)
            acc_ready = L.sig("acc_ready", FT, UR)
            acc_used = L.sig("acc_used", 2)
            units_q = [(0, "q0", 128, 2 * T, 0), (1, "q1", 64, T, 0)]
            FIRST_HEADS, HEADS, EARLY = 10, 5, 6

            def heads_before(i):
                return range(FIRST_HEADS + HEADS * (i - 1), FIRST_HEADS + HEADS * i) if i else range(FIRST_HEADS)

            def before(p):
                return p - 1 if isinstance(p, int) else (p, -1)

            def for_pairs(eng, body):
                body(0, ("first", 0), False, True)
                with eng.Fori(1, PAIRS - 1) as p:
                    body(p, ("loop", p), True, True)
                body(PAIRS - 1, ("last", PAIRS - 1), True, False)

            with nc.Block() as block:
                @block.sync
                def _(sp):
                    def load_keys(b, row):
                        load_stack(sp, kc[b], K_PARTS, [k2_scr[bass.ds(row, 1), c] for c in range(3)], k_loaded[b].sem)

                    def load_values(b, row):
                        sp.dma_start(vc[b][:].rearrange("p t c -> p (t c)"),
                                     v2_scr[bass.ds(row, 1)].rearrange("a p c -> p (a c)")).then_inc(v_loaded[b].sem, 16)

                    def store_q(s, row):
                        store_parts(sp, L, s, 0, 128, 2, T, [q2_scr[bass.ds(row, 1), c, 0:256] for c in range(3)])
                        store_parts(sp, L, s, 1, 64, 1, T, [q2_scr[bass.ds(row, 1), c, 256:D] for c in range(3)])

                    def load_q(s, row):
                        for st in L.stored:
                            sp.wait_ge(st.sem, st.at(s, 48))
                        load_stack(sp, L.qs, Q_PARTS, [q2_scr[bass.ds(row, 1), c] for c in range(3)], q_loaded.sem)

                    def store_out(q, row):
                        sp.wait_ge(acc_used.sem, acc_used.at(q, 2))
                        sp.dma_start(out[bass.ds(row, 2)].rearrange("b n d -> n b d"), x3b[:]).then_inc(out_stored.sem, 16)

                    load_x(sp, L, ln2, None, x1_scr[0:2])
                    load_xb(sp, L, x1_scr[0:2])
                    for b in range(2):
                        load_keys(b, b)
                        load_values(b, b)
                    store_q(0, 0)
                    load_q(0, 0)

                    def body(p, at, feed, stage):
                        if stage:
                            load_x(sp, L, ln2, p, x1_scr[bass.ds(2 * p + 2, 2)])
                        negmax_send(sp, L, at, "nm0", range(1))
                        negmax_send(sp, L, at, "nm1", range(1, 2))
                        if stage:
                            sp.wait_ge(L.st_ready.sem, L.st_ready.at(p, HG * JT))
                            load_keys(0, 2 * p + 2)
                            sp.wait_ge(L.pv_done.sem, L.pv_done.at(p, HG))
                            load_values(0, 2 * p + 2)
                            store_q((p, 1), p + 1)
                            sp.wait_ge(L.st_ready.sem, L.st_ready.at(p, 2 * HG * JT))
                            load_q((p, 1), p + 1)
                            load_keys(1, 2 * p + 3)
                            sp.wait_ge(L.pv_done.sem, L.pv_done.at(p, 2 * HG))
                            load_values(1, 2 * p + 3)
                            L.dense.wait_used(sp, at, "o1")
                            load_xb(sp, L, x1_scr[bass.ds(2 * p + 2, 2)])
                        if feed:
                            store_out(before(p), 2 * p - 2)

                    for_pairs(sp, body)
                    store_out(PAIRS - 1, B - 2)
                    sp.wait_ge(out_stored.sem, out_stored.at(PAIRS, 0))

                @block.tensor
                def _(pe):
                    def head_max(p, heads):
                        for m in heads:
                            b, h = divmod(m, H)
                            if m == H:
                                pe.wait_ge(k_loaded[1].sem, k_loaded[1].at(p, 96))
                            pe.wait_ge(L.max_used.sem, L.max_used.at(p, m - len(L.max_banks) + 1))
                            pe.matmul(ps[0:N, L.max_banks[m % len(L.max_banks)], 0:J], L.qs[0:STACK, h, b * N:b * N + N],
                                      kc[b][0:STACK, h, 0:J], start=True, stop=True).then_inc(L.max_ready.sem, 1)

                    def feed_up(at, i):
                        L.dense.wait_free(pe, at, f"f{i}")
                        for j in range(2):
                            for n, (xs, ws, rows) in enumerate(PASSES_D):
                                mm = pe.matmul(ps[:, L.dense.bank(at, f"f{i}"), j * T:j * T + T],
                                               r32(wf1[0:rows, ws, j * F + 128 * i:j * F + 128 * i + 128]),
                                               r32(h3T[0:rows, xs, :]), start=n == 0, stop=n == len(PASSES_D) - 1)
                        mm.then_inc(L.dense.ready.sem, 1)

                    def feed_down(q, t):
                        if t == 0:
                            pe.wait_ge(acc_used.sem, acc_used.at(q, 0))
                        pe.wait_ge(u_lo.sem, u_lo.at(q, t + 1))
                        for b in range(2):
                            for n, (us, ws) in enumerate([(0, 0), (1, 0), (0, 1)]):
                                mm = pe.matmul(ps[0:N, BK_ACC + b, 0:D], r32(uT[:, t % UR, us, b * N:b * N + N]),
                                               r32(wf2[:, t, ws, :]), start=t == 0 and n == 0, stop=t == FT - 1 and n == 2)
                        mm.then_inc(acc_ready.sem, 1)

                    def feed(q, at, i):
                        feed_up(at, i)
                        if i >= 2:
                            feed_down(q, i - 2)

                    def stage_norm(s, at):
                        ln_turn(pe, L, ln2, s, at, ("h0", "h1"))

                    def stage_q(s, at, i):
                        if i == 0:
                            pe.wait_ge(ln2.h_lo.sem, ln2.h_lo.at(s, 1))
                        cols_product(pe, L, at, f"q{i}", L.hT, wqo, [[(0, 128), (128, 128)], [(256, 64)]][i], PASSES_D)

                    stage_norm(0, ("pro", 0))
                    for i in range(2):
                        stage_q(0, ("pro", 0), i)

                    def body(p, at, fed, stage):
                        q = before(p)
                        pe.wait_ge(q_loaded.sem, q_loaded.at(p, 96))
                        pe.wait_ge(k_loaded[0].sem, k_loaded[0].at(p, 96))
                        for i in range(EARLY + 1):
                            head_max(p, heads_before(i))
                            if i == 4:
                                negmax_turn(pe, L, p, at, "nm0", range(1))
                            if fed:
                                if i == 0:
                                    pe.wait_ge(ln3.h_lo.sem, ln3.h_lo.at(q, 1))
                                feed_up(at, i)
                                if 2 <= i < EARLY:
                                    feed_down(q, i - 2)
                        negmax_turn(pe, L, p, at, "nm1", range(1, 2))
                        if fed:
                            feed_down(q, EARLY - 2)
                            feed(q, at, EARLY + 1)
                        else:
                            pe.wait_ge(ones_done.sem, 2)

                        def values(g):
                            if g % HG == 0:
                                pe.wait_ge(v_loaded[g // HG].sem, v_loaded[g // HG].at(p, 16))
                            for jt in range(JT):
                                values_pe(pe, L, p, g * JT + jt, vc[g // HG], JT, JW)

                        for g in range(2 * HG):
                            for jt in range(JT):
                                scores_pe(pe, L, p, g * JT + jt, kc[g // HG], JT, JW, 0)
                            if g == 3 and stage:
                                stage_norm((p, 1), at)
                            if g == HG + 1:
                                tail_turn(pe, L, p, 0, at)
                            if g == HG + 2:
                                tail_return(pe, L, 0, at)
                            if g:
                                values(g - 1)
                            if g in (HG + 1, HG + 2) and stage:
                                stage_q((p, 1), at, g - HG - 1)
                            if g == HG + 3:
                                tail_product(pe, L, 0, at, wqo, D)
                        values(2 * HG - 1)
                        if fed:
                            feed_up(at, 8)
                        tail_turn(pe, L, p, 1, at)
                        if fed:
                            feed_down(q, 6)
                        tail_return(pe, L, 1, at)
                        if fed:
                            feed_down(q, 7)
                        tail_product(pe, L, 1, at, wqo, D)
                        if fed:
                            feed_up(at, 9)
                            feed_down(q, 8)
                        ln_turn(pe, L, ln3, p, at, ("g0", "g1"))
                        if fed:
                            feed_down(q, 9)

                    for_pairs(pe, body)
                    pe.wait_ge(ln3.h_lo.sem, ln3.h_lo.at(PAIRS - 1, 1))
                    for i in range(FT):
                        feed(PAIRS - 1, ("epi", PAIRS), i)
                    feed_down(PAIRS - 1, FT - 2)
                    feed_down(PAIRS - 1, FT - 1)

                @block.scalar
                def _(act):
                    def gelu(q, at, i):
                        L.dense.wait_ready(act, at, f"f{i}")
                        if i >= 2:
                            L.dense.wait_used(act, at, f"f{i - 2}")
                        act.activation(gl[:, i % 2, :], ps[:, L.dense.bank(at, f"f{i}"), T:2 * T], ACT.Gelu,
                                       bias=b1c[:, FT + i:FT + i + 1]).then_inc(gelu_done.sem, 1)

                    def upper(q, at, i):
                        L.dense.wait_used(act, at, f"f{i}")
                        act.wait_ge(acc_ready.sem, acc_ready.at(q, i + 1 - UR))
                        act.copy(r32(uT[:, i % UR, 0, :]), uf[:, i % 2, :]).then_inc(u_hi.sem, 1)

                    def feed(q, at, i):
                        gelu(q, at, i)
                        if i:
                            upper(q, at, i - 1)

                    ln_hi(act, L, ln2, ("pro", 0), ("h0", "h1"), L.hT)
                    parts_act(act, L, 0, ("pro", 0), units_q)

                    def body(p, at, fed, stage):
                        q = before(p)
                        if fed:
                            for i in range(EARLY + 2):
                                feed(q, at, i)
                            upper(q, at, EARLY + 1)
                        for g in range(2 * HG):
                            exp_act(act, L, p, g, JT, JW)
                            if g == HG + 2:
                                tail_hi(act, L, p, 0, at)
                            if g:
                                values_act(act, L, p, g - 1)
                            if stage:
                                if g in (3, 4):
                                    ln_hi(act, L, ln2, at, ("h0", "h1"), L.hT, [g - 3])
                                if g in (HG + 2, HG + 3):
                                    part_second(act, L, (p, 1), at, *units_q[g - HG - 2])
                                if g in (HG + 1, HG + 2):
                                    part_first(act, L, (p, 1), at, *units_q[g - HG - 1])
                        values_act(act, L, p, 2 * HG - 1)
                        if fed:
                            gelu(q, at, 8)
                            upper(q, at, 8)
                        tail_hi(act, L, p, 1, at)
                        if fed:
                            gelu(q, at, 9)
                            upper(q, at, 9)
                        ln_hi(act, L, ln3, at, ("g0", "g1"), h3T)

                    for_pairs(act, body)
                    for i in range(FT):
                        feed(PAIRS - 1, ("epi", PAIRS), i)
                    upper(PAIRS - 1, ("epi", PAIRS), FT - 1)

                @block.vector
                def _(dve):
                    begin(dve, L)

                    def gate(q, at, i):
                        dve.wait_ge(gelu_done.sem, gelu_done.at(q, i + 1))
                        dve.wait_ge(u_lo.sem, u_lo.at(q, i - 1))
                        ins = dve.scalar_tensor_tensor(out=uf[:, i % 2, :], in0=ps[:, L.dense.bank(at, f"f{i}"), 0:T],
                                                       scalar=b1c[:, i:i + 1], in1=gl[:, i % 2, :], op0=ALU.add, op1=ALU.mult)
                        L.dense.release(ins, at, f"f{i}")

                    def add_out(q):
                        dve.wait_ge(acc_ready.sem, acc_ready.at(q, FT))
                        dve.wait_ge(x3b_done.sem, x3b_done.at(q, 1))
                        for b in range(2):
                            dve.tensor_tensor(x3b[:, b], ps[0:N, BK_ACC + b, 0:D], x3b[:, b], ALU.add).then_inc(acc_used.sem, 1)

                    def head_max(p, heads):
                        for m in heads:
                            max_dve(dve, L, p, m, 1, m // H, m % H, J)

                    dve.wait_ge(L.x_loaded.sem, L.x_loaded.at(0, 16))
                    ln_stats(dve, L, ln2, 0, 0, L.x, range(2))
                    ln_scale(dve, L, ln2, 0, 0, L.x, range(2))
                    ln_whole(dve, L, ln2, 0, ("pro", 0), ("h0", "h1"))
                    parts_dve(dve, L, 0, ("pro", 0), units_q)

                    def body(p, at, fed, stage):
                        q = before(p)
                        for i in range(EARLY + 1):
                            if i == 4:
                                negmax_dve(dve, L, p, 0, H)
                            head_max(p, heads_before(i))
                            if i == 4:
                                negmax_rows(dve, L, p, at, "nm0", range(1))
                            if i == EARLY:
                                negmax_dve(dve, L, p, 1, 2 * H)
                            if fed:
                                gate(q, at, i)
                        negmax_rows(dve, L, p, at, "nm1", range(1, 2))
                        if fed:
                            gate(q, at, EARLY + 1)
                        if stage:
                            dve.wait_ge(L.x_loaded.sem, L.x_loaded.at((p, 1), 16))
                            ln_stats(dve, L, ln2, (p, 1), 0, L.x, range(2))
                            ln_scale(dve, L, ln2, (p, 1), 0, L.x, range(2))
                            ln_whole(dve, L, ln2, (p, 1), at, ("h0", "h1"))
                        tail_divide(dve, L, p, 0, at)
                        if stage:
                            parts_dve(dve, L, (p, 1), at, units_q[:1])
                        tail_lo(dve, L, p, 0, at)
                        if stage:
                            parts_dve(dve, L, (p, 1), at, units_q[1:])
                        dve.wait_ge(x3b_done.sem, x3b_done.at(p, 0))
                        tail_add(dve, L, p, 0, at)
                        L.dense.wait_used(dve, at, "o0")
                        ln_stats(dve, L, ln3, p, 0, L.xo, range(1))
                        ln_scale(dve, L, ln3, p, 0, L.xo, range(1))
                        if fed:
                            gate(q, at, 8)
                        tail_divide(dve, L, p, 1, at)
                        tail_lo(dve, L, p, 1, at)
                        tail_add(dve, L, p, 1, at)
                        L.dense.wait_used(dve, at, "o1")
                        ln_stats(dve, L, ln3, p, 1, L.xo, range(1, 2))
                        ln_scale(dve, L, ln3, p, 1, L.xo, range(1, 2))
                        if fed:
                            gate(q, at, 9)
                        ln_whole(dve, L, ln3, p, at, ("g0", "g1"))
                        if fed:
                            add_out(q)

                    for_pairs(dve, body)
                    for i in range(FT):
                        gate(PAIRS - 1, ("epi", PAIRS), i)
                    add_out(PAIRS - 1)

                @block.gpsimd
                def _(pool):
                    def residual(q, last):
                        pool.wait_ge(out_stored.sem, out_stored.at(last, 16))
                        pool.tensor_tensor(x3b[:], L.xo[:], brow[:, 2:3, :].broadcast_to([N, 2, D]), ALU.add).then_inc(x3b_done.sem, 1)

                    def lower(q, tiles):
                        for i in tiles:
                            pool.wait_ge(u_hi.sem, u_hi.at(q, i + 1))
                            pool.tensor_tensor(r32(uT[:, i % UR, 1, :]), uf[:, i % 2, :], uT[:, i % UR, 0, :],
                                               ALU.subtract).then_inc(u_lo.sem, 1)

                    ln_rstd(pool, ln2, 0, 0, range(2))
                    ln_lo(pool, L, ln2, ("pro", 0), ("h0", "h1"), L.hT)
                    parts_pool(pool, L, 0, units_q)
                    pool.wait_ge(L.part2.sem, L.part2.at(0, 2))
                    for b in range(2):
                        pool.memset(kc[b][STACK:STACK + 2], 1.0).then_inc(ones_done.sem, 1)
                        pool.wait_ge(ones_done.sem, b + 1)

                    def body(p, at, fed, stage):
                        q = before(p)
                        if fed:
                            residual(q, (p, -2))
                        bias_add(pool, L, p, 1)
                        if fed:
                            lower(q, range(EARLY + 2))
                        if stage:
                            ln_rstd(pool, ln2, (p, 1), 0, range(2))
                            ln_lo(pool, L, ln2, at, ("h0", "h1"), L.hT)
                            parts_pool(pool, L, (p, 1), units_q)
                        ln_rstd(pool, ln3, p, 0, range(1))
                        if fed:
                            lower(q, range(EARLY + 2, FT - 1))
                        ln_rstd(pool, ln3, p, 1, range(1, 2))
                        if fed:
                            lower(q, range(FT - 1, FT))
                        ln_lo(pool, L, ln3, at, ("g0", "g1"), h3T)

                    for_pairs(pool, body)
                    residual(PAIRS - 1, PAIRS - 2)
                    lower(PAIRS - 1, range(FT))


def kernel(**inputs):
    import numpy as np
    import concourse.bacc as bacc
    from concourse.bass_utils import run_bass_kernel_spmd

    a = {n.replace("L0_xattn_", ""): np.asarray(v) for n, v in inputs.items()}

    def columns(v):
        return np.stack([v[0:128], v[128:256], np.concatenate([v[256:320], v[256:320]])], axis=1)

    ln_cols = np.stack([np.stack([columns(a[f"n{i}_g"]), columns(a[f"n{i}_b"])], axis=2) for i in (1, 2, 3)], axis=1)
    arrays = {
        "x": a["x"],
        "ctx_t": np.ascontiguousarray(a["ctx_768"].transpose(0, 2, 1)),
        **{n: a[n] for n in ("q1", "k1", "v1", "o1_w", "q2", "k2", "v2", "o2_w", "ff_w1", "ff_w2")},
        "ln_cols": np.ascontiguousarray(ln_cols.reshape(128, -1)),
        "b1_cols": np.ascontiguousarray(a["ff_b1"].reshape(2 * FT, 128).T),
        "bias_rows": np.ascontiguousarray(np.broadcast_to(
            np.concatenate([a["o1_b"], a["o2_b"], a["ff_b2"]])[None], (N, 3 * D))),
        "ident": np.eye(128, dtype=np.float32),
    }
    nc = bacc.Bacc("TRN2", target_bir_lowering=False, num_devices=1)
    args = [nc.dram_tensor(f"in_{n}", v.shape, mybir.dt.from_np(v.dtype), kind="ExternalInput").ap()
            for n, v in arrays.items()]
    out = nc.dram_tensor("out_0", (B, N, D), F32, kind="ExternalOutput").ap()
    build(nc, *args, out)
    r = run_bass_kernel_spmd(nc, [{f"in_{n}": v for n, v in arrays.items()}], core_ids=[0])
    return r.results[0]["out_0"]
```

```python
from contextlib import ExitStack

import concourse.bass as bass
from concourse import mybir

ALU = mybir.AluOpType
ACT = mybir.ActivationFunctionType
AX = mybir.AxisListType
F32 = mybir.dt.float32
F32R = mybir.dt.float32r
BF16 = mybir.dt.bfloat16

B, N, D = 16, 112, 320
H, DH = 20, 16
CTX, J = 192, 375
JP = J + 1
F = 4 * D
PAIRS = B // 2
T = 2 * N
HG = H // 4
JT, JW = 3, J // 3
KT = 3
FT = F // 128
STACK = 6 * DH
VW = DH + 1
EPS = 1e-05
SCALE = DH ** -0.5

PASSES_D = [(0, 0, 128), (1, 0, 128), (0, 1, 128), (2, 2, 128), (3, 2, 128), (2, 3, 128),
            (4, 4, 128), (5, 4, 64)]
PASSES_C = [(0, 0, 128), (1, 0, 128), (0, 1, 128), (2, 2, 128), (3, 2, 64)]
Q_PARTS = [0, 0, 0, 1, 1, 2]
K_PARTS = [0, 1, 2, 0, 1, 0]


def r32(ap):
    return ap.bitcast(F32R)


class Signal:

    def __init__(self, ctx, nc, name, per, lead=1):
        self.sem = ctx.enter_context(nc.semaphore(name))
        self.per, self.lead, self.given = per, lead, 0

    def at(self, p, k):
        if isinstance(p, tuple):
            p, offset = p
            k += offset * self.per
        return p * self.per + (k + self.lead)


class Loop:
    pass


class Norm:
    pass


class Weights:
    pass


class Ring:

    def __init__(self, ctx, nc, name, banks, parts):
        self.ready = Signal(ctx, nc, name + "_ready", 0)
        self.used = [Signal(ctx, nc, f"{name}_used{i}", 0) for i in range(len(banks))]
        self.banks = banks
        self.parts, start = {}, 0
        for kind, names, p0, count in parts:
            assert count == 1 or len(names) % len(banks) == 0
            self.parts[kind] = (start, names, p0)
            start += len(names) * count

    def number(self, at, name, every=1):
        kind, p = at
        start, names, p0 = self.parts[kind]
        n = (start + names.index(name)) // every
        return n if isinstance(p, int) and p == p0 else (p - p0) * (len(names) // every) + n

    def slot(self, at, name):
        start, names, _ = self.parts[at[0]]
        return (start + names.index(name)) % len(self.banks)

    def bank(self, at, name):
        return self.banks[self.slot(at, name)]

    def wait_free(self, eng, at, name):
        u = self.used[self.slot(at, name)]
        eng.wait_ge(u.sem, self.number(at, name, len(self.banks)) + u.lead)

    def wait_used(self, eng, at, name):
        u = self.used[self.slot(at, name)]
        eng.wait_ge(u.sem, self.number(at, name, len(self.banks)) + (1 + u.lead))

    def wait_ready(self, eng, at, name):
        eng.wait_ge(self.ready.sem, self.number(at, name) + (1 + self.ready.lead))

    def release(self, ins, at, name):
        ins.then_inc(self.used[self.slot(at, name)].sem, 1)


def build(nc, x, ctx_t, q1, k1, v1, o1, q2, k2, v2, o2, w1, w2, ln_cols, b1_cols, bias_rows, ident, out):
    top = ExitStack()
    with top:
        def dram(name, shape, dt):
            return nc.dram_tensor(name, shape, dt, kind="Internal").ap()

        qk_scr = dram("qk_scr", [PAIRS, 3, 2 * D, T], BF16)
        q2_scr = dram("q2_scr", [PAIRS, 3, D, T], BF16)
        k2_scr = dram("k2_scr", [B, 3, D, JP], BF16)
        v2_scr = dram("v2_scr", [B, JW, JT * H * VW], F32)
        x1_scr = dram("x1_scr", [B, N, D], F32)

        def sbt(ctx, name, shape, dt=F32):
            return ctx.enter_context(nc.sbuf_tensor(name, shape, dt))

        ps = top.enter_context(nc.psum_tensor("ps", [128, 8, 512], F32))
        eye = sbt(top, "eye", [128, 128])
        lnc = sbt(top, "lnc", [128, 3, KT, 2])
        b1c = sbt(top, "b1c", [128, 2 * FT])
        brow = sbt(top, "brow", [N, 3, D])
        neghalf = sbt(top, "neghalf", [N, 2])
        epsc = sbt(top, "epsc", [N, 2])

        const_loaded = Signal(top, nc, "const_loaded", 0, 0)

        def load_weights(sp, W, chunks, which):
            for i in which:
                kind, sources, w, c0, n = chunks[i]
                raw = W.raw[i]
                if i >= 2:
                    sp.wait_ge(W.lo.sem, i - 1)
                for src, at, m in sources:
                    if kind == "d":
                        views = [(raw[:, 0:2, at:at + m], src[0:256].rearrange("(k p) m -> p k m", p=128)),
                                 (raw[0:64, 2, at:at + m], src[256:320]), (raw[64:128, 2, at:at + m], src[256:320])]
                    elif kind == "c":
                        views = [(raw[:, 0, at:at + m], src[0:128]), (raw[0:64, 1, at:at + m], src[128:192]),
                                 (raw[64:128, 1, at:at + m], src[128:192])]
                    else:
                        flat = raw[:].rearrange("p a b -> p (a b)")[:, 0:n * D].rearrange("p (k m) -> p k m", m=D)
                        views = [(flat, src[c0 * 128:(c0 + n) * 128].rearrange("(k p) m -> p k m", p=128))]
                    for dst, s in views:
                        sp.dma_start(dst, s).then_inc(W.loaded[i].sem, 16)

        def split_hi(eng, copy, W, chunks, which):
            for i in which:
                kind, sources, w, c0, n = chunks[i]
                raw = W.raw[i]
                eng.wait_ge(W.loaded[i].sem, 16 * len(sources) * (1 if kind == "f" else 3))
                if kind == "d":
                    ins = copy(r32(w[:, 0:5:2, c0:c0 + n]), raw[:, 0:3, 0:n])
                elif kind == "c":
                    ins = copy(r32(w[:, 0:3:2, c0:c0 + n]), raw[:, 0:2, 0:n])
                else:
                    flat = raw[:].rearrange("p a b -> p (a b)")[:, 0:n * D].rearrange("p (k m) -> p k m", m=D)
                    ins = copy(r32(w[:, c0:c0 + n, 0]), flat)
                ins.then_inc(W.hi.sem, 1)

        def split_lo(eng, W, chunks, which):
            for i in which:
                kind, _, w, c0, n = chunks[i]
                raw = W.raw[i]
                eng.wait_ge(W.hi.sem, i + 1)
                c = slice(c0, c0 + n)
                if kind == "d":
                    eng.tensor_tensor(r32(w[:, 1:4:2, c]), raw[:, 0:2, 0:n], w[:, 0:3:2, c], ALU.subtract)
                    ins = eng.tensor_tensor(r32(w[64:128, 4, c]), raw[64:128, 2, 0:n], w[64:128, 4, c], ALU.subtract)
                elif kind == "c":
                    eng.tensor_tensor(r32(w[:, 1, c]), raw[:, 0, 0:n], w[:, 0, c], ALU.subtract)
                    ins = eng.tensor_tensor(r32(w[64:128, 2, c]), raw[64:128, 1, 0:n], w[64:128, 2, c], ALU.subtract)
                else:
                    flat = raw[:].rearrange("p a b -> p (a b)")[:, 0:n * D].rearrange("p (k m) -> p k m", m=D)
                    ins = eng.tensor_tensor(r32(w[:, c, 1]), flat, w[:, c, 0], ALU.subtract)
                ins.then_inc(W.lo.sem, 1)

        def ln_stats(dve, L, n, p, s, src, batches):
            for b in batches:
                ins = dve.bn_stats(n.stats[:, b, :], src[:, b, :])
            ins.then_inc(n.stats_done.sem, 1)
            dve.wait_ge(n.stats_done.sem, n.stats_done.at(p, s + 1))
            dve.memset(L.tick[:], 0.0)
            for b in batches:
                ins = dve.bn_aggr(n.mv[:, b, :], n.stats[:, b, :])
            ins.then_inc(n.aggr_done.sem, 1)

        def ln_scale(dve, L, n, p, s, src, batches):
            dve.wait_ge(n.rstd_done.sem, n.rstd_done.at(p, s + 1))
            for b in batches:
                ins = dve.tensor_scalar(L.z[:, b, 0:D], src[:, b, :], n.mv[:, b, 0:1], n.rstd[:, b:b + 1],
                                        ALU.subtract, ALU.mult)
            ins.then_inc(n.z_done.sem, 1)

        def ln_rstd(pool, n, p, s, batches):
            c = slice(batches[0], batches[-1] + 1)
            pool.wait_ge(n.aggr_done.sem, n.aggr_done.at(p, s + 1))
            pool.tensor_tensor(n.ve[:, c], n.mv[:, c, 1], epsc[:, c], ALU.add).then_inc(n.var_done.sem, 1)
            pool.wait_ge(n.var_done.sem, n.var_done.at(p, s + 1))
            pool.tensor_tensor(n.rstd[:, c], n.ve[:, c], neghalf[:, c], ALU.pow).then_inc(n.rstd_done.sem, 1)

        def turned(uses):
            return list(zip(uses, [(0, 1), (2,)] if len(uses) == 2 else [(0,), (1,), (2,)]))

        def ln_turn(pe, L, n, p, at, uses):
            pe.wait_ge(n.z_done.sem, n.z_done.at(p, n.z_done.per))
            for use, tiles in turned(uses):
                L.dense.wait_free(pe, at, use)
                for i, kt in enumerate(tiles):
                    for b in range(2):
                        c = i * T + b * N
                        mm = pe.transpose(ps[:, L.dense.bank(at, use), c:c + N], L.z[:, b, 128 * kt:128 * kt + 128], eye[0:N, 0:N])
                mm.then_inc(L.dense.ready.sem, 1)

        def ln_hi(act, L, n, at, uses, hT, which=None):
            for use, tiles in turned(uses) if which is None else [turned(uses)[i] for i in which]:
                L.dense.wait_ready(act, at, use)
                bank = L.dense.bank(at, use)
                for i, kt in enumerate(tiles):
                    if kt < 2:
                        ins = act.activation(r32(hT[:, 2 * kt, :]), ps[:, bank, i * T:i * T + T], ACT.Identity,
                                             scale=lnc[:, n.norm, kt, 0:1], bias=lnc[:, n.norm, kt, 1:2])
                    else:
                        for half in range(2):
                            ins = act.activation(r32(hT[64 * half:64 * half + 64, 4, :]), ps[0:64, bank, 0:T], ACT.Identity,
                                                 scale=lnc[0:64, n.norm, 2, 0:1], bias=lnc[0:64, n.norm, 2, 1:2])
                ins.then_inc(n.h_hi.sem, 1)

        def ln_whole(dve, L, n, p, at, uses):
            for u, (use, tiles) in enumerate(turned(uses)):
                dve.wait_ge(n.h_hi.sem, n.h_hi.at(p, u + 1))
                for i, kt in enumerate(tiles):
                    rows = min(128, D - 128 * kt)
                    ins = dve.tensor_scalar(L.h[0:rows, kt, :], ps[0:rows, L.dense.bank(at, use), i * T:i * T + T],
                                            lnc[0:rows, n.norm, kt, 0:1], lnc[0:rows, n.norm, kt, 1:2], ALU.mult, ALU.add)
                L.dense.release(ins, at, use)

        def ln_lo(pool, L, n, at, uses, hT):
            for use, tiles in turned(uses):
                L.dense.wait_used(pool, at, use)
                for kt in tiles:
                    rows = min(128, D - 128 * kt)
                    ins = pool.tensor_tensor(r32(hT[0:rows, 2 * kt + 1, :]), L.h[0:rows, kt, :], hT[0:rows, 2 * kt, :], ALU.subtract)
            ins.then_inc(n.h_lo.sem, 1)

        def part_first(act, L, p, at, u, use, rows, cols, stored):
            L.dense.wait_ready(act, at, use)
            st = L.stored[u % len(L.stored)]
            act.wait_ge(st.sem, st.at(p, stored))
            act.copy(L.parts[u % len(L.stored)][0:rows, 0, 0:cols], ps[0:rows, L.dense.bank(at, use), 0:cols])\
               .then_inc(L.part0.sem, 1)

        def part_second(act, L, p, at, u, use, rows, cols, stored):
            L.dense.wait_used(act, at, use)
            act.copy(L.parts[u % len(L.stored)][0:rows, 1, 0:cols], L.rest[u % len(L.stored)][0:rows, 0:cols])\
               .then_inc(L.part1.sem, 1)

        def parts_act(act, L, p, at, units):
            for i, unit in enumerate(units):
                part_first(act, L, p, at, *unit)
                if i:
                    part_second(act, L, p, at, *units[i - 1])
            part_second(act, L, p, at, *units[-1])

        def parts_dve(dve, L, p, at, units):
            for u, use, rows, cols, _ in units:
                dve.wait_ge(L.part0.sem, L.part0.at(p, u + 1))
                dve.wait_ge(L.part2.sem, L.part2.at(p, u + 1 - len(L.stored)))
                slot = u % len(L.stored)
                ins = dve.tensor_tensor(L.rest[slot][0:rows, 0:cols], ps[0:rows, L.dense.bank(at, use), 0:cols],
                                        L.parts[slot][0:rows, 0, 0:cols], ALU.subtract)
                L.dense.release(ins, at, use)

        def parts_pool(pool, L, p, units):
            for u, _, rows, cols, _ in units:
                pool.wait_ge(L.part1.sem, L.part1.at(p, u + 1))
                slot = u % len(L.stored)
                pool.tensor_tensor(L.parts[slot][0:rows, 2, 0:cols], L.rest[slot][0:rows, 0:cols],
                                   L.parts[slot][0:rows, 1, 0:cols], ALU.subtract).then_inc(L.part2.sem, 1)

        def store_parts(sp, L, p, u, rows, tiles, cols, dst):
            slot = u % len(L.stored)
            sp.wait_ge(L.part2.sem, L.part2.at(p, u + 1))
            for c in range(3):
                src = L.parts[slot][0:rows, c, 0:tiles * cols]
                if tiles > 1:
                    src = src.rearrange("p (m t) -> p m t", m=tiles)
                    d = dst[c].rearrange("a (m p) t -> p (a m) t", p=128)
                else:
                    d = dst[c].rearrange("a p t -> p (a t)")
                sp.dma_start(d, src).then_inc(L.stored[slot].sem, 16)

        def load_stack(sp, stack, parts, src, sem):
            for g, c in enumerate(parts):
                sp.dma_start(stack[DH * g:DH * g + DH], src[c].rearrange("a (h d) t -> d (a h) t", d=DH)).then_inc(sem, 16)

        def max_dve(dve, L, p, m, heads, b, h0, width):
            dve.wait_ge(L.max_ready.sem, L.max_ready.at(p, m + 1))
            src = ps[0:N, L.max_banks[m % len(L.max_banks)], 0:heads * width]
            if heads > 1:
                src = src.rearrange("p (h j) -> p h j", h=heads)
            dve.tensor_reduce(L.mx[:, b, h0:h0 + heads], src, AX.X, ALU.max).then_inc(L.max_used.sem, 1)

        def negmax_dve(dve, L, p, b, m_done):
            dve.wait_ge(L.max_used.sem, L.max_used.at(p, m_done))
            dve.tensor_scalar(L.nm_hi[:, b, :], L.mx[:, b, :], -1.0, None, ALU.mult).then_inc(L.nm_hi_done.sem, 1)
            dve.wait_ge(L.nm_hi_done.sem, L.nm_hi_done.at(p, b + 1))
            dve.tensor_copy(L.nm[:, b, 0:H], L.nm_hi[:, b, :])
            dve.scalar_tensor_tensor(out=L.nm[:, b, H:2 * H], in0=L.mx[:, b, :], scalar=-1.0, in1=L.nm_hi[:, b, :],
                                     op0=ALU.mult, op1=ALU.subtract).then_inc(L.nm_done.sem, 1)

        def negmax_turn(pe, L, p, b, bank, wait_free, ready):
            pe.wait_ge(L.nm_done.sem, L.nm_done.at(p, b + 1))
            wait_free(pe)
            pe.transpose(ps[:, bank, 0:N], L.nm[:, b, :], eye[0:N, 0:N]).then_inc(ready.sem, 1)

        def negmax_rows(dve, L, p, b, bank, wait_ready, used):
            wait_ready(dve)
            dve.wait_ge(L.nmrow_loaded[b].sem, L.nmrow_loaded[b].at(p, 0))
            dve.tensor_copy(L.nmrow[:, b, :], ps[0:2 * H, bank, 0:N]).then_inc(used.sem, 1)

        def negmax_send(sp, L, b, wait_used):
            wait_used(sp)
            for i in range(2):
                sp.dma_start(L.qs[STACK + i:STACK + i + 1, :, b * N:b * N + N], L.nmrow[i * H:i * H + H, b, :])\
                  .then_inc(L.nmrow_loaded[b].sem, 16)

        def scores_pe(pe, L, p, i, ks, tiles, keys, keys_at):
            g, jt = divmod(i, tiles)
            b, hg = divmod(g, HG)
            if hg == 0 and jt == 0:
                pe.wait_ge(L.nmrow_loaded[b].sem, L.nmrow_loaded[b].at(p, 32))
            pe.wait_ge(L.exp_done.sem, L.exp_done.at(p, i + 1 - len(L.st_banks)))
            for hh in range(4):
                k0 = keys_at + jt * keys
                mm = pe.matmul(ps[0:keys, L.st_banks[i % len(L.st_banks)], hh * N:hh * N + N], ks[0:STACK + 2, 4 * hg + hh, k0:k0 + keys],
                               L.qs[0:STACK + 2, 4 * hg + hh, b * N:b * N + N], start=True, stop=True)
            mm.then_inc(L.st_ready.sem, 1)

        def exp_act(act, L, p, g, tiles, keys):
            act.wait_ge(L.pv_done.sem, L.pv_done.at(p, g - 1))
            for jt in range(tiles):
                i = g * tiles + jt
                act.wait_ge(L.st_ready.sem, L.st_ready.at(p, i + 1))
                act.activation(L.probs[0:keys, i % (2 * tiles), :], ps[0:keys, L.st_banks[i % len(L.st_banks)], 0:4 * N], ACT.Exp,
                               scale=SCALE).then_inc(L.exp_done.sem, 1)

        def values_pe(pe, L, p, i, values, tiles, keys):
            g, jt = divmod(i, tiles)
            if jt == 0:
                pe.wait_ge(L.ot_done.sem, L.ot_done.at(p, g + 1 - len(L.pv_banks)))
            pe.wait_ge(L.exp_done.sem, L.exp_done.at(p, i + 1))
            for hh in range(4):
                h = 4 * (g % HG) + hh
                mm = pe.matmul(ps[32 * hh:32 * hh + VW, L.pv_banks[g % len(L.pv_banks)], 0:N], values[0:keys, jt, h * VW:(h + 1) * VW],
                               L.probs[0:keys, i % (2 * tiles), hh * N:hh * N + N], start=jt == 0, stop=jt == tiles - 1)
            if jt == tiles - 1:
                mm.then_inc(L.pv_done.sem, 1)

        def values_act(act, L, p, g):
            b, hg = divmod(g, HG)
            act.wait_ge(L.pv_done.sem, L.pv_done.at(p, g + 1))
            act.copy(L.ot[:, b, hg * N:hg * N + N], ps[:, L.pv_banks[g % len(L.pv_banks)], 0:N]).then_inc(L.ot_done.sem, 1)

        def tail_turn(pe, L, p, b, at):
            pe.wait_ge(L.ot_done.sem, L.ot_done.at(p, HG * (b + 1)))
            for use, groups in ((f"t{b}a", range(4)), (f"t{b}b", range(4, HG))):
                L.dense.wait_free(pe, at, use)
                for i, hg in enumerate(groups):
                    mm = pe.transpose(ps[0:N, L.dense.bank(at, use), 128 * i:128 * i + 128], L.ot[:, b, hg * N:hg * N + N], eye[:, :])
                mm.then_inc(L.dense.ready.sem, 1)

        def tail_divide(dve, L, p, b, at):
            for half, (use, h0, heads) in enumerate([(f"t{b}a", 0, 16), (f"t{b}b", 16, 4)]):
                L.dense.wait_ready(dve, at, use)
                src = ps[0:N, L.dense.bank(at, use), 0:heads * 32].rearrange("p (h c) -> p h c", c=32)
                dve.reciprocal(L.rsum[:, h0:h0 + heads], src[:, :, DH]).then_inc(L.rsum_done.sem, 1)
                dve.wait_ge(L.rsum_done.sem, L.rsum_done.at(p, 2 * b + half + 1))
                ins = dve.tensor_tensor(L.on[:, h0 * DH:(h0 + heads) * DH].rearrange("p (h d) -> p h d", d=DH), src[:, :, 0:DH],
                                        L.rsum[:, h0:h0 + heads].unsqueeze(2).broadcast_to([N, heads, DH]), ALU.mult)
                L.dense.release(ins, at, use)

        def tail_return(pe, L, b, at):
            use = f"t{b}c"
            L.dense.wait_free(pe, at, use)
            L.dense.wait_used(pe, at, f"t{b}b")
            for kt in range(KT):
                rows = min(128, D - 128 * kt)
                mm = pe.transpose(ps[0:rows, L.dense.bank(at, use), kt * N:kt * N + N], L.on[:, 128 * kt:128 * kt + rows], eye[0:N, 0:N])
            mm.then_inc(L.dense.ready.sem, 1)

        def tail_hi(act, L, p, b, at):
            L.dense.wait_ready(act, at, f"t{b}c")
            bank = L.dense.bank(at, f"t{b}c")
            act.copy(r32(L.onT[:, 0:3:2, :]), ps[:, bank, 0:2 * N].rearrange("p (k t) -> p k t", k=2))
            for half in range(2):
                ins = act.copy(r32(L.onT[64 * half:64 * half + 64, 4, :]), ps[0:64, bank, 2 * N:3 * N])
            ins.then_inc(L.on_hi.sem, 1)

        def tail_lo(dve, L, p, b, at):
            dve.wait_ge(L.on_hi.sem, L.on_hi.at(p, b + 1))
            bank = L.dense.bank(at, f"t{b}c")
            dve.tensor_tensor(r32(L.onT[:, 1:4:2, :]), ps[:, bank, 0:2 * N].rearrange("p (k t) -> p k t", k=2),
                              L.onT[:, 0:3:2, :], ALU.subtract)
            ins = dve.tensor_tensor(r32(L.onT[0:64, 5, :]), ps[0:64, bank, 2 * N:3 * N], L.onT[0:64, 4, :], ALU.subtract)
            L.dense.release(ins, at, f"t{b}c")

        def tail_product(pe, L, b, at, w, w0):
            L.dense.wait_used(pe, at, f"t{b}c")
            rows_product(pe, L, at, f"o{b}", L.onT, 0, N, w, w0, PASSES_D)

        def tail_add(dve, L, p, b, at):
            L.dense.wait_ready(dve, at, f"o{b}")
            dve.wait_ge(L.xb_done.sem, L.xb_done.at(p, 1))
            ins = dve.tensor_tensor(L.xo[:, b], ps[0:N, L.dense.bank(at, f"o{b}"), 0:D], L.xb[:, b], ALU.add)
            L.dense.release(ins, at, f"o{b}")

        def rows_product(pe, L, at, use, xT, c0, tokens, w, w0, passes):
            L.dense.wait_free(pe, at, use)
            for i, (xs, ws, rows) in enumerate(passes):
                mm = pe.matmul(ps[0:tokens, L.dense.bank(at, use), 0:D], r32(xT[0:rows, xs, c0:c0 + tokens]),
                               r32(w[0:rows, ws, w0:w0 + D]), start=i == 0, stop=i == len(passes) - 1)
            mm.then_inc(L.dense.ready.sem, 1)

        def cols_product(pe, L, at, use, xT, w, blocks, passes):
            L.dense.wait_free(pe, at, use)
            width = xT.shape[2]
            for j, (w0, m) in enumerate(blocks):
                for i, (xs, ws, rows) in enumerate(passes):
                    mm = pe.matmul(ps[0:m, L.dense.bank(at, use), j * width:j * width + width], r32(w[0:rows, ws, w0:w0 + m]),
                                   r32(xT[0:rows, xs, :]), start=i == 0, stop=i == len(passes) - 1)
            mm.then_inc(L.dense.ready.sem, 1)

        def common(ctx, tag, dense_parts, parts_per, slots, slot_stores, maxima, banks, tiles, part_cols):
            L = Loop()
            L.signals = []

            def sig(name, per, lead=1):
                s = Signal(ctx, nc, f"{tag}_{name}", per, lead)
                L.signals.append(s)
                return s

            def norm(number, calls, uses=2):
                n = Norm()
                n.norm = number
                name = f"ln{number}_"
                n.stats_done = sig(name + "stats_done", calls)
                n.aggr_done = sig(name + "aggr_done", calls)
                n.var_done = sig(name + "var_done", calls)
                n.rstd_done = sig(name + "rstd_done", calls)
                n.z_done = sig(name + "z_done", calls)
                n.h_hi = sig(name + "h_hi", uses)
                n.h_lo = sig(name + "h_lo", 1)
                n.stats = sbt(ctx, tag + name + "stats", [N, 2, 6])
                n.mv = sbt(ctx, tag + name + "mv", [N, 2, 2])
                n.ve = sbt(ctx, tag + name + "ve", [N, 2])
                n.rstd = sbt(ctx, tag + name + "rstd", [N, 2])
                return n

            L.sig, L.norm = sig, norm
            L.begun = Signal(ctx, nc, tag + "_begun", 0, 0)
            L.st_banks, L.max_banks, L.pv_banks, dense_banks = banks
            L.dense = Ring(ctx, nc, tag + "_dense", dense_banks, dense_parts)
            L.signals += [L.dense.ready, *L.dense.used]
            L.part0 = sig("part0", parts_per)
            L.part1 = sig("part1", parts_per)
            L.part2 = sig("part2", parts_per, slots)
            L.stored = [Signal(ctx, nc, f"{tag}_stored{i}", slot_stores) for i in range(slots)]
            L.signals += L.stored
            L.max_ready = sig("max_ready", maxima)
            L.max_used = sig("max_used", maxima, 4)
            L.nm_hi_done = sig("nm_hi_done", 2)
            L.nm_done = sig("nm_done", 2)
            L.on_hi = sig("on_hi", 2)
            L.rsum_done = sig("rsum_done", 4)
            L.nmrow_loaded = [sig(f"nmrow_loaded{b}", 32) for b in range(2)]
            L.st_ready = sig("st_ready", 2 * HG * tiles)
            L.exp_done = sig("exp_done", 2 * HG * tiles, 3)
            L.pv_done = sig("pv_done", 2 * HG, 2)
            L.ot_done = sig("ot_done", 2 * HG, 2)
            L.x_loaded = sig("x_loaded", 16)
            L.xb_loaded = sig("xb_loaded", 16)
            L.xb_done = sig("xb_done", 1)
            L.tick = sbt(ctx, tag + "_tick", [1, 2])
            L.x = sbt(ctx, tag + "_x", [N, 2, D])
            L.xb = sbt(ctx, tag + "_xb", [N, 2, D])
            L.xo = sbt(ctx, tag + "_xo", [N, 2, D])
            L.z = sbt(ctx, tag + "_z", [N, 2, 128 * KT])
            L.h = sbt(ctx, tag + "_h", [128, KT, T])
            L.hT = sbt(ctx, tag + "_hT", [128, 6, T])
            L.parts = [sbt(ctx, f"{tag}_parts{i}", [128, 3, part_cols], BF16) for i in range(slots)]
            L.rest = [sbt(ctx, f"{tag}_rest{i}", [128, part_cols]) for i in range(slots)]
            L.qs = sbt(ctx, tag + "_qs", [STACK + 2, H, T], BF16)
            L.mx = sbt(ctx, tag + "_mx", [N, 2, H])
            L.nm_hi = sbt(ctx, tag + "_nm_hi", [N, 2, H], BF16)
            L.nm = sbt(ctx, tag + "_nm", [N, 2, 128])
            L.nmrow = sbt(ctx, tag + "_nmrow", [2 * H, 2, N], BF16)
            L.probs = sbt(ctx, tag + "_probs", [128, 2 * tiles, 4 * N])
            L.ot = sbt(ctx, tag + "_ot", [128, 2, HG * N])
            L.rsum = sbt(ctx, tag + "_rsum", [N, H])
            L.on = sbt(ctx, tag + "_on", [N, D])
            L.onT = sbt(ctx, tag + "_onT", [128, 6, N])
            return L

        def begin(eng, L):
            for s in L.signals:
                eng.sem_inc(s.sem, s.lead + s.given)
            eng.memset(ps[:, L.pv_banks[0]:L.pv_banks[-1] + 1, 0:N], 0.0)
            eng.memset(L.z[:], 0.0)
            eng.memset(L.nm[:], 0.0).then_inc(L.begun.sem, 1)

        def load_x(sp, L, n, before, src):
            if before is not None:
                sp.wait_ge(n.z_done.sem, n.z_done.at(before, 1))
            sp.dma_start(L.x[:], src.rearrange("b n d -> n b d")).then_inc(L.x_loaded.sem, 16)

        def load_xb(sp, L, src):
            sp.dma_start(L.xb[:], src.rearrange("b n d -> n b d")).then_inc(L.xb_loaded.sem, 16)

        def bias_add(pool, L, p, row):
            pool.wait_ge(L.xb_loaded.sem, L.xb_loaded.at(p, 16))
            pool.tensor_tensor(L.xb[:], L.xb[:], brow[:, row:row + 1, :].broadcast_to([N, 2, D]), ALU.add).then_inc(L.xb_done.sem, 1)

        def overlay(name, names):
            with ExitStack() as ctx:
                return [sbt(ctx, f"{name}{i}", [128, 3, 2 * D]) for i in names]

        wqo = sbt(top, "wqo", [128, 5, 2 * D])
        raw_first = overlay("raw_first", (0, 1))
        wf1 = sbt(top, "wf1", [128, 5, 2 * F])
        wf2 = sbt(top, "wf2", [128, FT, 2, D])

        with ExitStack() as ctx:
            CONTEXT = [[f"c{b}{kind}{m}" for kind in "kv" for m in range(3)] for b in range(2)]
            BODY = ["h0", "h1", "h2", "c1k2", "c1v0", "c1v1", "c1v2", "qk0", "qk1", "qk2", "c0k0", "c0k1", "c0k2", "c0v0",
                    "c0v1", "c0v2", "t0a", "t0b", "v0", "t0c", "o0", "t1a", "t1b", "v1", "c1k0", "t1c", "c1k1", "o1"]
            LAST = ["h0", "h1", "h2", "c1k2", "c1v0", "c1v1", "c1v2", "q0", "q1", "t0a", "t0b", "t0c", "o0", "t1a", "t1b", "t1c", "o1"]
            STAGE = ["h0", "h1", "h2", "qk0", "qk1", "qk2", "v0", "v1"] + CONTEXT[0] + CONTEXT[1][0:2]
            L = common(ctx, "a", [("pro", STAGE, 0, 1), ("loop", BODY, 0, PAIRS - 2),
                                  ("late", BODY, PAIRS - 2, 1), ("last", LAST, PAIRS - 1, 1)],
                       9, 3, 16 * 9, 2 * HG + 2, ((0, 1), (2, 3, 0, 1), (2, 3), (4, 5, 6, 7)), 1, 2 * T)
            ln1, ln2 = L.norm(0, 1, 3), L.norm(1, 1, 3)

            TURN = HG + 1
            turn_slot = (TURN + 1, 2 * HG + 1)

            def max_slot(g):
                return g + (g > TURN)

            def turn_bank(b):
                return L.max_banks[turn_slot[b] % len(L.max_banks)]
            raw_rest = overlay("raw_rest", (0,))
            wqk = sbt(ctx, "wqk", [128, 5, 2 * D])
            raw_rest += overlay("raw_rest", (1,))
            wkv = sbt(ctx, "wkv", [128, 3, 2 * D])
            wvo = sbt(ctx, "wvo", [128, 5, 2 * D])
            chunks = [("d", [(q1, 0, D), (k1, D, D)], wqk, 0, 2 * D),
                      ("d", [(v1, 0, D), (o1, D, D)], wvo, 0, 2 * D),
                      ("c", [(k2, 0, D), (v2, D, D)], wkv, 0, 2 * D),
                      ("d", [(q2, 0, D), (o2, D, D)], wqo, 0, 2 * D)]
            chunks += [("d", [(w1[:, c:c + 2 * D], 0, 2 * D)], wf1, c, 2 * D) for c in range(0, 2 * F, 2 * D)]
            chunks += [("f", [(w2, 0, D)], wf2, 0, 6), ("f", [(w2, 0, D)], wf2, 6, FT - 6)]
            FIRST, REST = range(3), range(3, len(chunks))
            W = Weights()
            W.raw = [(raw_first if i in FIRST else raw_rest)[(i - 3) % 2] for i in range(len(chunks))]
            W.loaded = [Signal(ctx, nc, f"w_loaded{i}", 0, 0) for i in range(len(chunks))]
            W.hi = Signal(ctx, nc, "w_hi", 0, 0)
            W.lo = Signal(ctx, nc, "w_lo", 0, 0)

            ks = sbt(ctx, "a_ks", [STACK + 2, H, T], BF16)
            ctxr = sbt(ctx, "ctxr", [128, 2, JP])
            ctxT = sbt(ctx, "ctxT", [128, 4, JP])
            va = sbt(ctx, "va", [N, 2, H * VW])
            vc = sbt(ctx, "vc", [JW, 2, JT, H * VW])
            init_done = Signal(ctx, nc, "init_done", 0, 0)
            ks_ones = Signal(ctx, nc, "ks_ones", 0, 0)
            ctx_loaded = L.sig("ctx_loaded", 96)
            ctx_hi = L.sig("ctx_hi", 2)
            ctx_lo = L.sig("ctx_lo", 2)
            stack_loaded = L.sig("stack_loaded", 16 * 12)
            vc_stored = [L.sig(f"vc_stored{b}", 16) for b in range(2)]
            xo_stored = L.sig("xo_stored", 16)

            units_qk = [(u, f"qk{u}", 128, 2 * T if u < 2 else T, 0) for u in range(3)]
            units_q = [(0, "q0", 128, 2 * T, 0), (1, "q1", 64, T, 0)]
            units_k2 = [[(3 + 3 * b + m, f"c{b}k{m}", min(128, D - 128 * m), JP, 48 * (b + 1)) for m in range(KT)]
                        for b in range(2)]

            with nc.Block() as block:
                @block.sync
                def _(sp):
                    load_x(sp, L, ln1, None, x[0:2])
                    for dst, src in ((eye, ident), (lnc, ln_cols), (b1c, b1_cols), (brow, bias_rows)):
                        d = dst[:]
                        if len(dst.shape) > 2:
                            d = d.rearrange("p a b c -> p (a b c)" if len(dst.shape) == 4 else "p a b -> p (a b)")
                        sp.dma_start(d, src).then_inc(const_loaded.sem, 16)

                    def load_ctx(c):
                        for dst, lo, hi in ((ctxr[:, 0, 0:J], 0, 128), (ctxr[0:64, 1, 0:J], 128, CTX), (ctxr[64:128, 1, 0:J], 128, CTX)):
                            sp.dma_start(dst, c[:, lo:hi].rearrange("a c t -> c (a t)")).then_inc(ctx_loaded.sem, 16)

                    def store_qk(s, row, units):
                        for u, tiles, r0 in [((0, 2, 0), (1, 2, 256), (2, 1, 512))[u] for u in units]:
                            store_parts(sp, L, s, u, 128, tiles, T,
                                        [qk_scr[bass.ds(row, 1), c, r0:r0 + 128 * tiles] for c in range(3)])

                    def wait_stored(s, count):
                        for st in L.stored:
                            sp.wait_ge(st.sem, st.at(s, count))

                    def load_stacks(row):
                        load_stack(sp, L.qs, Q_PARTS, [qk_scr[bass.ds(row, 1), c, 0:D] for c in range(3)], stack_loaded.sem)
                        load_stack(sp, ks, K_PARTS, [qk_scr[bass.ds(row, 1), c, D:2 * D] for c in range(3)], stack_loaded.sem)

                    load_weights(sp, W, chunks, FIRST)
                    sp.wait_ge(init_done.sem, 1)
                    load_ctx(ctx_t[0:1])
                    load_x(sp, L, ln1, 0, x[2:4])
                    load_xb(sp, L, x[0:2])
                    sp.wait_ge(ctx_lo.sem, ctx_lo.at(0, 1))
                    load_ctx(ctx_t[1:2])

                    def store_keys(s, b, tiles, row):
                        for m in tiles:
                            store_parts(sp, L, s, 3 + 3 * b + m, min(128, D - 128 * m), 1, JP,
                                        [k2_scr[bass.ds(row, 1), c, 128 * m:min(D, 128 * m + 128)] for c in range(3)])

                    def store_values(at, b, row):
                        L.dense.wait_used(sp, at, f"c{b}v2")
                        sp.dma_start(v2_scr[bass.ds(row, 1)].rearrange("a p c -> p (a c)"),
                                     vc[:, b].rearrange("p t c -> p (t c)")).then_inc(vc_stored[b].sem, 16)

                    store_qk(0, 0, range(3))
                    wait_stored(0, 48)
                    load_stacks(0)
                    store_keys(0, 0, range(3), 0)
                    store_values(("pro", 0), 0, 0)
                    store_keys(0, 1, range(2), 1)

                    def send(p, b):
                        negmax_send(sp, L, b, lambda e: e.wait_ge(L.max_used.sem, L.max_used.at(p, turn_slot[b] + 1)))

                    def body(p, at):
                        stage = at[0] != "last"
                        if stage:
                            sp.wait_ge(ctx_lo.sem, ctx_lo.at(p, 2))
                            load_ctx(ctx_t[bass.ds(2 * p + 2, 1)])
                        else:
                            load_weights(sp, W, chunks, REST[:1])
                        store_keys(p, 1, range(2, 3), 2 * p + 1)
                        store_values(at, 1, 2 * p + 1)
                        if at[0] == "loop":
                            load_x(sp, L, ln1, (p, 1), x[bass.ds(2 * p + 4, 2)])
                        elif at[0] == "late":
                            sp.wait_ge(xo_stored.sem, xo_stored.at(1, 0))
                            load_x(sp, L, ln1, (p, 1), x1_scr[0:2])
                        if not stage:
                            load_weights(sp, W, chunks, REST[1:2])
                        send(p, 0)
                        if stage:
                            store_qk((p, 1), p + 1, range(2))
                        send(p, 1)
                        if stage:
                            store_qk((p, 1), p + 1, range(2, 3))
                            sp.wait_ge(ctx_lo.sem, ctx_lo.at((p, 1), 1))
                            load_ctx(ctx_t[bass.ds(2 * p + 3, 1)])
                            store_keys((p, 1), 0, range(3), 2 * p + 2)
                            store_values(at, 0, 2 * p + 2)
                            sp.wait_ge(L.st_ready.sem, L.st_ready.at(p, 2 * HG))
                            wait_stored((p, 1), 96)
                            load_stacks(p + 1)
                            store_keys((p, 1), 1, range(2), 2 * p + 3)
                        else:
                            load_weights(sp, W, chunks, REST[2:4])
                            store_parts(sp, L, PAIRS, 0, 128, 2, T, [q2_scr[0:1, c, 0:256] for c in range(3)])
                            store_parts(sp, L, PAIRS, 1, 64, 1, T, [q2_scr[0:1, c, 256:D] for c in range(3)])
                            load_weights(sp, W, chunks, REST[4:])
                        L.dense.wait_used(sp, at, "o1")
                        sp.dma_start(x1_scr[bass.ds(2 * p, 2)].rearrange("b n d -> n b d"), L.xo[:]).then_inc(xo_stored.sem, 16)
                        if stage:
                            load_xb(sp, L, x[bass.ds(2 * p + 2, 2)])

                    with sp.Fori(0, PAIRS - 2) as p:
                        body(p, ("loop", p))
                    body(PAIRS - 2, ("late", PAIRS - 2))
                    body(PAIRS - 1, ("last", PAIRS - 1))
                    for i, s in enumerate([*L.stored, *vc_stored, xo_stored]):
                        sp.wait_ge(s.sem, s.at(PAIRS, 48 if i < 2 else 0))

                @block.tensor
                def _(pe):
                    def stage_norm(s, at):
                        ln_turn(pe, L, ln1, s, at, ("h0", "h1", "h2"))

                    def stage_qk(s, at, i):
                        if i == 0:
                            pe.wait_ge(ln1.h_lo.sem, ln1.h_lo.at(s, 1))
                        blocks = ([(0, 128), (128, 128)], [(256, 128), (384, 128)], [(512, 128)])[i]
                        cols_product(pe, L, at, f"qk{i}", L.hT, wqk, blocks, PASSES_D)

                    def stage_v(at, b):
                        rows_product(pe, L, at, f"v{b}", L.hT, b * N, N, wvo, 0, PASSES_D)

                    def context(p, at, b, i):
                        if i == 0:
                            pe.wait_ge(ctx_lo.sem, ctx_lo.at(p, b + 1))
                        if i < KT:
                            cols_product(pe, L, at, CONTEXT[b][i], ctxT, wkv, [(128 * i, min(128, D - 128 * i))], PASSES_C)
                        else:
                            rows_product(pe, L, at, CONTEXT[b][i], ctxT, (i - KT) * JW, JW, wkv, D, PASSES_C)

                    def group_max(p, g):
                        (b, hg), m = divmod(g, HG), max_slot(g)
                        pe.wait_ge(L.max_used.sem, L.max_used.at(p, m - len(L.max_banks) + 1))
                        for hh in range(4):
                            t = slice(b * N, b * N + N)
                            mm = pe.matmul(ps[0:N, L.max_banks[m % len(L.max_banks)], hh * N:hh * N + N], L.qs[0:STACK, 4 * hg + hh, t],
                                           ks[0:STACK, 4 * hg + hh, t], start=True, stop=True)
                        mm.then_inc(L.max_ready.sem, 1)

                    def turn(p, b):
                        k = turn_slot[b] - len(L.max_banks) + 1
                        negmax_turn(pe, L, p, b, turn_bank(b), lambda e: e.wait_ge(L.max_used.sem, L.max_used.at(p, k)), L.max_ready)

                    pe.wait_ge(const_loaded.sem, 64)
                    pe.wait_ge(init_done.sem, 1)
                    pe.wait_ge(ks_ones.sem, 1)
                    pe.wait_ge(L.begun.sem, 1)
                    stage_norm(0, ("pro", 0))
                    pe.wait_ge(W.lo.sem, 1)
                    for i in range(3):
                        stage_qk(0, ("pro", 0), i)
                    pe.wait_ge(W.lo.sem, 2)
                    for b in range(2):
                        stage_v(("pro", 0), b)
                    pe.wait_ge(W.lo.sem, 3)
                    for i in range(6):
                        context(0, ("pro", 0), 0, i)
                    for i in range(2):
                        context(0, ("pro", 0), 1, i)

                    def body(p, at):
                        stage = at[0] != "last"
                        if stage:
                            stage_norm((p, 1), at)
                        else:
                            ln_turn(pe, L, ln2, 0, at, ("h0", "h1", "h2"))
                        for i in range(2, 6):
                            context(p, at, 1, i)
                        pe.wait_ge(stack_loaded.sem, stack_loaded.at(p, stack_loaded.per))
                        for g in range(2 * HG):
                            group_max(p, g)
                            if g == TURN:
                                turn(p, 0)
                            if stage and g in (3, 5, 7):
                                stage_qk((p, 1), at, (g - 3) // 2)
                        if stage:
                            context((p, 1), at, 0, 0)
                        turn(p, 1)
                        if stage:
                            for i in range(1, 3):
                                context((p, 1), at, 0, i)
                        pe.wait_ge(L.max_used.sem, L.max_used.at(p, L.max_used.per))
                        for g in range(2 * HG):
                            scores_pe(pe, L, p, g, ks, 1, N, (g // HG) * N)
                            if g in (2, 3) and not stage:
                                if g == 2:
                                    pe.wait_ge(ln2.h_lo.sem, ln2.h_lo.at(0, 1))
                                    pe.wait_ge(W.lo.sem, REST[0] + 1)
                                cols_product(pe, L, at, f"q{g - 2}", L.hT, wqo, [[(0, 128), (128, 128)], [(256, 64)]][g - 2], PASSES_D)
                            if 2 <= g <= 4 and stage:
                                context((p, 1), at, 0, g + 1)
                            if g == HG + 1:
                                tail_turn(pe, L, p, 0, at)
                                if stage:
                                    stage_v(at, 0)
                            if g == HG + 2:
                                tail_return(pe, L, 0, at)
                            if g == HG + 3:
                                tail_product(pe, L, 0, at, wvo, D)
                            if g:
                                values_pe(pe, L, p, g - 1, va[:, (g - 1) // HG:(g - 1) // HG + 1], 1, N)
                        values_pe(pe, L, p, 2 * HG - 1, va[:, 1:2], 1, N)
                        tail_turn(pe, L, p, 1, at)
                        if stage:
                            stage_v(at, 1)
                            context((p, 1), at, 1, 0)
                        tail_return(pe, L, 1, at)
                        if stage:
                            context((p, 1), at, 1, 1)
                        tail_product(pe, L, 1, at, wvo, D)

                    with pe.Fori(0, PAIRS - 2) as p:
                        body(p, ("loop", p))
                    body(PAIRS - 2, ("late", PAIRS - 2))
                    body(PAIRS - 1, ("last", PAIRS - 1))

                @block.scalar
                def _(act):
                    def context_hi(p, b):
                        act.wait_ge(ctx_loaded.sem, ctx_loaded.at(p, 48 * (b + 1)))
                        act.copy(r32(ctxT[:, 0:3:2, :]), ctxr[:, :, :]).then_inc(ctx_hi.sem, 1)

                    def context_values(p, at, b, tiles):
                        act.wait_ge(vc_stored[b].sem, vc_stored[b].at(p, 0))
                        for jt in tiles:
                            L.dense.wait_ready(act, at, f"c{b}v{jt}")
                            ins = act.copy(vc[:, b, jt].rearrange("p (h c) -> p h c", c=VW)[:, :, 0:DH],
                                           ps[0:JW, L.dense.bank(at, f"c{b}v{jt}"), 0:D].rearrange("p (h d) -> p h d", d=DH))
                            L.dense.release(ins, at, f"c{b}v{jt}")

                    def stage_values(at, b):
                        L.dense.wait_ready(act, at, f"v{b}")
                        ins = act.copy(va[:, b].rearrange("p (h c) -> p h c", c=VW)[:, :, 0:DH],
                                       ps[0:N, L.dense.bank(at, f"v{b}"), 0:D].rearrange("p (h d) -> p h d", d=DH))
                        L.dense.release(ins, at, f"v{b}")

                    act.wait_ge(const_loaded.sem, 64)
                    act.wait_ge(init_done.sem, 1)
                    split_hi(act, act.copy, W, chunks, range(1))
                    ln_hi(act, L, ln1, ("pro", 0), ("h0", "h1", "h2"), L.hT)
                    split_hi(act, act.copy, W, chunks, range(1, 3))
                    context_hi(0, 0)
                    parts_act(act, L, 0, ("pro", 0), units_qk)
                    for b in range(2):
                        stage_values(("pro", 0), b)
                    parts_act(act, L, 0, ("pro", 0), units_k2[0])
                    context_values(0, ("pro", 0), 0, range(JT))
                    context_hi(0, 1)
                    parts_act(act, L, 0, ("pro", 0), units_k2[1][:2])

                    def body(p, at):
                        stage = at[0] != "last"
                        if stage:
                            ln_hi(act, L, ln1, at, ("h0", "h1", "h2"), L.hT)
                        else:
                            ln_hi(act, L, ln2, at, ("h0", "h1", "h2"), L.hT)
                        parts_act(act, L, p, at, units_k2[1][2:])
                        context_values(p, at, 1, range(JT))
                        if stage:
                            context_hi((p, 1), 0)
                            parts_act(act, L, (p, 1), at, units_qk)
                        else:
                            split_hi(act, act.copy, W, chunks, REST[:2])
                        for g in range(2 * HG):
                            exp_act(act, L, p, g, 1, N)
                            if not stage and g in (3, 4):
                                part_second(act, L, PAIRS, at, *units_q[g - 3])
                            if not stage and g in (2, 3):
                                part_first(act, L, PAIRS, at, *units_q[g - 2])
                            if stage:
                                if 2 <= g <= 4:
                                    part_second(act, L, (p, 1), at, *units_k2[0][g - 2])
                                if 1 <= g <= 3:
                                    part_first(act, L, (p, 1), at, *units_k2[0][g - 1])
                                if 4 <= g <= 6:
                                    context_values((p, 1), at, 0, range(g - 4, g - 3))
                                if g == HG + 3:
                                    context_hi((p, 1), 1)
                                if g == HG + 1:
                                    stage_values(at, 0)
                            if g == HG + 2:
                                tail_hi(act, L, p, 0, at)
                            if g:
                                values_act(act, L, p, g - 1)
                        values_act(act, L, p, 2 * HG - 1)
                        if stage:
                            stage_values(at, 1)
                            part_first(act, L, (p, 1), at, *units_k2[1][0])
                        tail_hi(act, L, p, 1, at)
                        if stage:
                            part_second(act, L, (p, 1), at, *units_k2[1][0])
                            parts_act(act, L, (p, 1), at, units_k2[1][1:2])

                    with act.Fori(0, PAIRS - 2) as p:
                        body(p, ("loop", p))
                    body(PAIRS - 2, ("late", PAIRS - 2))
                    body(PAIRS - 1, ("last", PAIRS - 1))
                    act.wait_ge(W.hi.sem, REST[4])
                    split_hi(act, act.copy, W, chunks, REST[4:])

                @block.vector
                def _(dve):
                    begin(dve, L)
                    dve.wait_ge(const_loaded.sem, 64)
                    dve.wait_ge(init_done.sem, 1)
                    dve.wait_ge(L.x_loaded.sem, L.x_loaded.at(0, 16))
                    ln_stats(dve, L, ln1, 0, 0, L.x, range(2))
                    ln_scale(dve, L, ln1, 0, 0, L.x, range(2))
                    split_lo(dve, W, chunks, range(1))
                    ln_whole(dve, L, ln1, 0, ("pro", 0), ("h0", "h1", "h2"))
                    split_lo(dve, W, chunks, range(1, 3))
                    parts_dve(dve, L, 0, ("pro", 0), units_qk)
                    dve.wait_ge(L.x_loaded.sem, L.x_loaded.at(1, 16))
                    ln_stats(dve, L, ln1, 1, 0, L.x, range(2))
                    parts_dve(dve, L, 0, ("pro", 0), units_k2[0])
                    ln_scale(dve, L, ln1, 1, 0, L.x, range(2))
                    parts_dve(dve, L, 0, ("pro", 0), units_k2[1][:2])

                    def body(p, at):
                        stage, far = at[0] != "last", at[0] == "loop"
                        if stage:
                            ln_whole(dve, L, ln1, (p, 1), at, ("h0", "h1", "h2"))
                        else:
                            ln_whole(dve, L, ln2, 0, at, ("h0", "h1", "h2"))
                        parts_dve(dve, L, p, at, units_k2[1][2:])
                        for g in range(2 * HG):
                            max_dve(dve, L, p, max_slot(g), 4, g // HG, 4 * (g % HG), N)
                            if g % HG == HG - 1:
                                negmax_dve(dve, L, p, g // HG, max_slot(g) + 1)
                            if g == TURN:
                                rows(p, 0)
                            if stage and g in (5, 7):
                                parts_dve(dve, L, (p, 1), at, [units_qk[(g - 5) // 2]])
                        rows(p, 1)
                        if stage:
                            parts_dve(dve, L, (p, 1), at, units_qk[2:])
                            parts_dve(dve, L, (p, 1), at, units_k2[0])
                        else:
                            split_lo(dve, W, chunks, REST[:2])
                            parts_dve(dve, L, PAIRS, at, units_q)
                        n, s = (ln1, (p, 2)) if far else (ln2, 0)
                        if stage:
                            dve.wait_ge(L.x_loaded.sem, L.x_loaded.at((p, 2), 16))
                            ln_stats(dve, L, n, s, 0, L.x, range(2))
                        dve.wait_ge(xo_stored.sem, xo_stored.at(p, 0))
                        tail_divide(dve, L, p, 0, at)
                        if stage:
                            ln_scale(dve, L, n, s, 0, L.x, range(2))
                        tail_lo(dve, L, p, 0, at)
                        if not stage:
                            split(REST[2:3])
                        tail_add(dve, L, p, 0, at)
                        tail_divide(dve, L, p, 1, at)
                        if stage:
                            parts_dve(dve, L, (p, 1), at, units_k2[1][:1])
                        tail_lo(dve, L, p, 1, at)
                        if stage:
                            parts_dve(dve, L, (p, 1), at, units_k2[1][1:2])
                        else:
                            split(REST[3:4])
                        tail_add(dve, L, p, 1, at)

                    def rows(p, b):
                        m = turn_slot[b]
                        negmax_rows(dve, L, p, b, turn_bank(b), lambda e: e.wait_ge(L.max_ready.sem, L.max_ready.at(p, m + 1)), L.max_used)

                    def split(which):
                        for i in which:
                            split_hi(dve, dve.tensor_copy, W, chunks, [i])
                            split_lo(dve, W, chunks, [i])

                    with dve.Fori(0, PAIRS - 2) as p:
                        body(p, ("loop", p))
                    body(PAIRS - 2, ("late", PAIRS - 2))
                    body(PAIRS - 1, ("last", PAIRS - 1))
                    split_lo(dve, W, chunks, REST[4:])

                @block.gpsimd
                def _(pool):
                    pool.memset(neghalf[:], -0.5)
                    pool.memset(epsc[:], EPS)
                    pool.memset(ctxr[:], 0.0)
                    pool.memset(va[:], 1.0)
                    pool.memset(vc[:], 1.0).then_inc(init_done.sem, 1)
                    pool.wait_ge(init_done.sem, 1)
                    pool.memset(ks[STACK:STACK + 2], 1.0).then_inc(ks_ones.sem, 1)
                    pool.wait_ge(ks_ones.sem, 1)
                    pool.wait_ge(const_loaded.sem, 64)

                    def context_lo(p, b):
                        pool.wait_ge(ctx_hi.sem, ctx_hi.at(p, b + 1))
                        pool.tensor_tensor(r32(ctxT[:, 1, :]), ctxr[:, 0, :], ctxT[:, 0, :], ALU.subtract)
                        pool.tensor_tensor(r32(ctxT[0:64, 3, :]), ctxr[0:64, 1, :], ctxT[0:64, 2, :], ALU.subtract)\
                            .then_inc(ctx_lo.sem, 1)

                    ln_rstd(pool, ln1, 0, 0, range(2))
                    ln_lo(pool, L, ln1, ("pro", 0), ("h0", "h1", "h2"), L.hT)
                    context_lo(0, 0)
                    parts_pool(pool, L, 0, units_qk)
                    ln_rstd(pool, ln1, 1, 0, range(2))
                    parts_pool(pool, L, 0, units_k2[0])
                    context_lo(0, 1)
                    parts_pool(pool, L, 0, units_k2[1][:2])

                    def body(p, at):
                        stage = at[0] != "last"
                        if stage:
                            ln_lo(pool, L, ln1, at, ("h0", "h1", "h2"), L.hT)
                        else:
                            ln_lo(pool, L, ln2, at, ("h0", "h1", "h2"), L.hT)
                        parts_pool(pool, L, p, units_k2[1][2:])
                        if stage:
                            context_lo((p, 1), 0)
                            parts_pool(pool, L, (p, 1), units_qk)
                        bias_add(pool, L, p, 0)
                        if not stage:
                            parts_pool(pool, L, PAIRS, units_q)
                        if stage:
                            parts_pool(pool, L, (p, 1), units_k2[0])
                            if at[0] == "loop":
                                ln_rstd(pool, ln1, (p, 2), 0, range(2))
                            else:
                                ln_rstd(pool, ln2, 0, 0, range(2))
                            context_lo((p, 1), 1)
                            parts_pool(pool, L, (p, 1), units_k2[1][:2])

                    with pool.Fori(0, PAIRS - 2) as p:
                        body(p, ("loop", p))
                    body(PAIRS - 2, ("late", PAIRS - 2))
                    body(PAIRS - 1, ("last", PAIRS - 1))

        with ExitStack() as ctx:
            BODY = ["f0", "f1", "f2", "f3", "nm0", "f4", "f5", "f6", "nm1", "f7", "h0", "h1", "t0a", "t0b", "q0", "t0c", "q1",
                    "o0", "f8", "t1a", "t1b", "t1c", "o1", "f9", "g0", "g1"]
            STAGE = ["h0", "h1", "q0", "q1"]
            FEED = [f"f{i}" for i in range(FT)]
            L = common(ctx, "c", [("first", [n for n in BODY if n not in FEED], 0, 1),
                                  ("loop", BODY, 1, PAIRS - 2), ("last", [n for n in BODY if n not in STAGE], PAIRS - 1, 1),
                                  ("epi", FEED, PAIRS, 1)],
                       2, 2, 48, 2 * H, ((0, 1, 4), (5, 0, 1, 4), (5,), (6, 7)), JT, 2 * T)
            ln2, ln3 = L.norm(1, 1), L.norm(2, 2)
            BK_ACC = 2
            h3T = sbt(ctx, "h3T", [128, 6, T])
            x3b = sbt(ctx, "x3b", [N, 2, D])
            gl = sbt(ctx, "gl", [128, 2, T])
            uf = sbt(ctx, "uf", [128, 2, T])
            UR = 5
            uT = sbt(ctx, "uT", [128, UR, 2, T])
            kc = [sbt(ctx, f"kc{b}", [STACK + 2, H, JP], BF16) for b in range(2)]
            vc = [sbt(ctx, f"vcc{b}", [JW, JT, H * VW]) for b in range(2)]
            for s in (ln2.stats_done, ln2.aggr_done, ln2.var_done, ln2.rstd_done, ln2.z_done, ln2.h_hi, ln2.h_lo,
                      L.x_loaded, L.part0, L.part1, L.part2, *L.stored):
                s.given = s.per
            ones_done = Signal(ctx, nc, "ones_done", 0, 0)
            x3b_done = L.sig("x3b_done", 1)
            k_loaded = [L.sig(f"k_loaded{b}", 96) for b in range(2)]
            v_loaded = [L.sig(f"v_loaded{b}", 16) for b in range(2)]
            q_loaded = L.sig("q_loaded", 96)
            out_stored = L.sig("out_stored", 16)
            gelu_done = L.sig("gelu_done", FT)
            u_hi = L.sig("u_hi", FT)
            u_lo = L.sig("u_lo", FT, 2)
            acc_ready = L.sig("acc_ready", FT, UR)
            acc_used = L.sig("acc_used", 2)
            units_q = [(0, "q0", 128, 2 * T, 0), (1, "q1", 64, T, 0)]
            HEADS = (6, 6, 6, 6, 6, 5, 5)
            EARLY = len(HEADS) - 1

            def heads_before(i):
                return range(sum(HEADS[:i]), sum(HEADS[:i + 1]))

            def before(p):
                return p - 1 if isinstance(p, int) else (p, -1)

            def for_pairs(eng, body):
                body(0, ("first", 0), False, True)
                with eng.Fori(1, PAIRS - 1) as p:
                    body(p, ("loop", p), True, True)
                body(PAIRS - 1, ("last", PAIRS - 1), True, False)

            with nc.Block() as block:
                @block.sync
                def _(sp):
                    def load_keys(b, row):
                        load_stack(sp, kc[b], K_PARTS, [k2_scr[bass.ds(row, 1), c] for c in range(3)], k_loaded[b].sem)

                    def load_values(b, row):
                        sp.dma_start(vc[b][:].rearrange("p t c -> p (t c)"),
                                     v2_scr[bass.ds(row, 1)].rearrange("a p c -> p (a c)")).then_inc(v_loaded[b].sem, 16)

                    def store_q(s, row):
                        store_parts(sp, L, s, 0, 128, 2, T, [q2_scr[bass.ds(row, 1), c, 0:256] for c in range(3)])
                        store_parts(sp, L, s, 1, 64, 1, T, [q2_scr[bass.ds(row, 1), c, 256:D] for c in range(3)])

                    def load_q(s, row):
                        for st in L.stored:
                            sp.wait_ge(st.sem, st.at(s, 48))
                        load_stack(sp, L.qs, Q_PARTS, [q2_scr[bass.ds(row, 1), c] for c in range(3)], q_loaded.sem)

                    def store_out(q, row):
                        sp.wait_ge(acc_used.sem, acc_used.at(q, 2))
                        sp.dma_start(out[bass.ds(row, 2)].rearrange("b n d -> n b d"), x3b[:]).then_inc(out_stored.sem, 16)

                    load_q(0, 0)
                    load_keys(0, 0)
                    load_keys(1, 1)
                    for b in range(2):
                        load_values(b, b)
                    load_xb(sp, L, x1_scr[0:2])

                    def body(p, at, feed, stage):
                        if stage:
                            load_x(sp, L, ln2, p, x1_scr[bass.ds(2 * p + 2, 2)])
                        for b in range(2):
                            negmax_send(sp, L, b, lambda e: L.dense.wait_used(e, at, f"nm{b}"))
                        if stage:
                            sp.wait_ge(L.st_ready.sem, L.st_ready.at(p, HG * JT))
                            load_keys(0, 2 * p + 2)
                            sp.wait_ge(L.pv_done.sem, L.pv_done.at(p, HG))
                            load_values(0, 2 * p + 2)
                            store_q((p, 1), p + 1)
                            sp.wait_ge(L.st_ready.sem, L.st_ready.at(p, 2 * HG * JT))
                            load_q((p, 1), p + 1)
                            load_keys(1, 2 * p + 3)
                            sp.wait_ge(L.pv_done.sem, L.pv_done.at(p, 2 * HG))
                            load_values(1, 2 * p + 3)
                            L.dense.wait_used(sp, at, "o1")
                            load_xb(sp, L, x1_scr[bass.ds(2 * p + 2, 2)])
                        if feed:
                            store_out(before(p), 2 * p - 2)

                    for_pairs(sp, body)
                    store_out(PAIRS - 1, B - 2)
                    sp.wait_ge(out_stored.sem, out_stored.at(PAIRS, 0))

                @block.tensor
                def _(pe):
                    def head_max(p, heads):
                        for m in heads:
                            b, h = divmod(m, H)
                            if m == H:
                                pe.wait_ge(k_loaded[1].sem, k_loaded[1].at(p, 96))
                            pe.wait_ge(L.max_used.sem, L.max_used.at(p, m - len(L.max_banks) + 1))
                            pe.matmul(ps[0:N, L.max_banks[m % len(L.max_banks)], 0:J], L.qs[0:STACK, h, b * N:b * N + N],
                                      kc[b][0:STACK, h, 0:J], start=True, stop=True).then_inc(L.max_ready.sem, 1)

                    def turn(p, at, b):
                        use = f"nm{b}"
                        negmax_turn(pe, L, p, b, L.dense.bank(at, use), lambda e: L.dense.wait_free(e, at, use), L.dense.ready)

                    def feed_up(at, i):
                        L.dense.wait_free(pe, at, f"f{i}")
                        for j in range(2):
                            for n, (xs, ws, rows) in enumerate(PASSES_D):
                                mm = pe.matmul(ps[:, L.dense.bank(at, f"f{i}"), j * T:j * T + T],
                                               r32(wf1[0:rows, ws, j * F + 128 * i:j * F + 128 * i + 128]),
                                               r32(h3T[0:rows, xs, :]), start=n == 0, stop=n == len(PASSES_D) - 1)
                        mm.then_inc(L.dense.ready.sem, 1)

                    def feed_down(q, t):
                        if t == 0:
                            pe.wait_ge(acc_used.sem, acc_used.at(q, 0))
                        pe.wait_ge(u_lo.sem, u_lo.at(q, t + 1))
                        for b in range(2):
                            for n, (us, ws) in enumerate([(0, 0), (1, 0), (0, 1)]):
                                mm = pe.matmul(ps[0:N, BK_ACC + b, 0:D], r32(uT[:, t % UR, us, b * N:b * N + N]),
                                               r32(wf2[:, t, ws, :]), start=t == 0 and n == 0, stop=t == FT - 1 and n == 2)
                        mm.then_inc(acc_ready.sem, 1)

                    def feed(q, at, i):
                        feed_up(at, i)
                        if i >= 2:
                            feed_down(q, i - 2)

                    def stage_norm(s, at):
                        ln_turn(pe, L, ln2, s, at, ("h0", "h1"))

                    def stage_q(s, at, i):
                        if i == 0:
                            pe.wait_ge(ln2.h_lo.sem, ln2.h_lo.at(s, 1))
                        cols_product(pe, L, at, f"q{i}", L.hT, wqo, [[(0, 128), (128, 128)], [(256, 64)]][i], PASSES_D)

                    pe.wait_ge(L.begun.sem, 1)

                    def body(p, at, fed, stage):
                        q = before(p)
                        pe.wait_ge(q_loaded.sem, q_loaded.at(p, 96))
                        pe.wait_ge(k_loaded[0].sem, k_loaded[0].at(p, 96))
                        for i in range(EARLY + 1):
                            head_max(p, heads_before(i))
                            if i == 4:
                                turn(p, at, 0)
                            if fed:
                                if i == 0:
                                    pe.wait_ge(ln3.h_lo.sem, ln3.h_lo.at(q, 1))
                                feed_up(at, i)
                                if 2 <= i < EARLY:
                                    feed_down(q, i - 2)
                        turn(p, at, 1)
                        if fed:
                            feed_down(q, EARLY - 2)
                            feed(q, at, EARLY + 1)
                        else:
                            pe.wait_ge(ones_done.sem, 2)

                        def values(g):
                            if g % HG == 0:
                                pe.wait_ge(v_loaded[g // HG].sem, v_loaded[g // HG].at(p, 16))
                            for jt in range(JT):
                                values_pe(pe, L, p, g * JT + jt, vc[g // HG], JT, JW)

                        for g in range(2 * HG):
                            for jt in range(JT):
                                scores_pe(pe, L, p, g * JT + jt, kc[g // HG], JT, JW, 0)
                            if g == 3 and stage:
                                stage_norm((p, 1), at)
                            if g == HG + 1:
                                tail_turn(pe, L, p, 0, at)
                            if g == HG + 2:
                                tail_return(pe, L, 0, at)
                            if g:
                                values(g - 1)
                            if g in (HG + 1, HG + 2) and stage:
                                stage_q((p, 1), at, g - HG - 1)
                            if g == HG + 3:
                                tail_product(pe, L, 0, at, wqo, D)
                        values(2 * HG - 1)
                        if fed:
                            feed_up(at, 8)
                        tail_turn(pe, L, p, 1, at)
                        if fed:
                            feed_down(q, 6)
                        tail_return(pe, L, 1, at)
                        if fed:
                            feed_down(q, 7)
                        tail_product(pe, L, 1, at, wqo, D)
                        if fed:
                            feed_up(at, 9)
                            feed_down(q, 8)
                        ln_turn(pe, L, ln3, p, at, ("g0", "g1"))
                        if fed:
                            feed_down(q, 9)

                    for_pairs(pe, body)
                    pe.wait_ge(ln3.h_lo.sem, ln3.h_lo.at(PAIRS - 1, 1))
                    for i in range(FT):
                        feed(PAIRS - 1, ("epi", PAIRS), i)
                    feed_down(PAIRS - 1, FT - 2)
                    feed_down(PAIRS - 1, FT - 1)

                @block.scalar
                def _(act):
                    def gelu(q, at, i):
                        L.dense.wait_ready(act, at, f"f{i}")
                        if i >= 2:
                            L.dense.wait_used(act, at, f"f{i - 2}")
                        act.activation(gl[:, i % 2, :], ps[:, L.dense.bank(at, f"f{i}"), T:2 * T], ACT.Gelu,
                                       bias=b1c[:, FT + i:FT + i + 1]).then_inc(gelu_done.sem, 1)

                    def upper(q, at, i):
                        L.dense.wait_used(act, at, f"f{i}")
                        act.wait_ge(acc_ready.sem, acc_ready.at(q, i + 1 - UR))
                        act.copy(r32(uT[:, i % UR, 0, :]), uf[:, i % 2, :]).then_inc(u_hi.sem, 1)

                    def feed(q, at, i):
                        gelu(q, at, i)
                        if i:
                            upper(q, at, i - 1)

                    def body(p, at, fed, stage):
                        q = before(p)
                        if fed:
                            for i in range(EARLY + 1):
                                feed(q, at, i)
                            gelu(q, at, EARLY + 1)
                        for g in range(2 * HG):
                            exp_act(act, L, p, g, JT, JW)
                            if g == 0 and fed:
                                for i in range(EARLY, EARLY + 2):
                                    upper(q, at, i)
                            if g == HG + 2:
                                tail_hi(act, L, p, 0, at)
                            if g:
                                values_act(act, L, p, g - 1)
                            if stage:
                                if g in (3, 4):
                                    ln_hi(act, L, ln2, at, ("h0", "h1"), L.hT, [g - 3])
                                if g in (HG + 2, HG + 3):
                                    part_second(act, L, (p, 1), at, *units_q[g - HG - 2])
                                if g in (HG + 1, HG + 2):
                                    part_first(act, L, (p, 1), at, *units_q[g - HG - 1])
                        values_act(act, L, p, 2 * HG - 1)
                        if fed:
                            gelu(q, at, 8)
                            upper(q, at, 8)
                        tail_hi(act, L, p, 1, at)
                        if fed:
                            gelu(q, at, 9)
                            upper(q, at, 9)
                        ln_hi(act, L, ln3, at, ("g0", "g1"), h3T)

                    for_pairs(act, body)
                    for i in range(FT):
                        feed(PAIRS - 1, ("epi", PAIRS), i)
                    upper(PAIRS - 1, ("epi", PAIRS), FT - 1)

                @block.vector
                def _(dve):
                    begin(dve, L)

                    def rows(p, at, b):
                        use = f"nm{b}"
                        negmax_rows(dve, L, p, b, L.dense.bank(at, use), lambda e: L.dense.wait_ready(e, at, use),
                                    L.dense.used[L.dense.slot(at, use)])

                    def gate(q, at, i):
                        dve.wait_ge(gelu_done.sem, gelu_done.at(q, i + 1))
                        dve.wait_ge(u_lo.sem, u_lo.at(q, i - 1))
                        ins = dve.scalar_tensor_tensor(out=uf[:, i % 2, :], in0=ps[:, L.dense.bank(at, f"f{i}"), 0:T],
                                                       scalar=b1c[:, i:i + 1], in1=gl[:, i % 2, :], op0=ALU.add, op1=ALU.mult)
                        L.dense.release(ins, at, f"f{i}")

                    def add_out(q):
                        dve.wait_ge(acc_ready.sem, acc_ready.at(q, FT))
                        dve.wait_ge(x3b_done.sem, x3b_done.at(q, 1))
                        for b in range(2):
                            dve.tensor_tensor(x3b[:, b], ps[0:N, BK_ACC + b, 0:D], x3b[:, b], ALU.add).then_inc(acc_used.sem, 1)

                    def head_max(p, heads):
                        for m in heads:
                            max_dve(dve, L, p, m, 1, m // H, m % H, J)

                    def body(p, at, fed, stage):
                        q = before(p)
                        for i in range(EARLY + 1):
                            if i == 4:
                                negmax_dve(dve, L, p, 0, H)
                            head_max(p, heads_before(i))
                            if i == 4:
                                rows(p, at, 0)
                            if i == EARLY:
                                negmax_dve(dve, L, p, 1, 2 * H)
                            if fed:
                                gate(q, at, i)
                        rows(p, at, 1)
                        if fed:
                            gate(q, at, EARLY + 1)
                        if stage:
                            dve.wait_ge(L.x_loaded.sem, L.x_loaded.at((p, 1), 16))
                            ln_stats(dve, L, ln2, (p, 1), 0, L.x, range(2))
                            ln_scale(dve, L, ln2, (p, 1), 0, L.x, range(2))
                            ln_whole(dve, L, ln2, (p, 1), at, ("h0", "h1"))
                        tail_divide(dve, L, p, 0, at)
                        if stage:
                            parts_dve(dve, L, (p, 1), at, units_q[:1])
                        tail_lo(dve, L, p, 0, at)
                        if stage:
                            parts_dve(dve, L, (p, 1), at, units_q[1:])
                        dve.wait_ge(x3b_done.sem, x3b_done.at(p, 0))
                        tail_add(dve, L, p, 0, at)
                        L.dense.wait_used(dve, at, "o0")
                        ln_stats(dve, L, ln3, p, 0, L.xo, range(1))
                        ln_scale(dve, L, ln3, p, 0, L.xo, range(1))
                        if fed:
                            gate(q, at, 8)
                        tail_divide(dve, L, p, 1, at)
                        tail_lo(dve, L, p, 1, at)
                        tail_add(dve, L, p, 1, at)
                        L.dense.wait_used(dve, at, "o1")
                        ln_stats(dve, L, ln3, p, 1, L.xo, range(1, 2))
                        ln_scale(dve, L, ln3, p, 1, L.xo, range(1, 2))
                        if fed:
                            gate(q, at, 9)
                        ln_whole(dve, L, ln3, p, at, ("g0", "g1"))
                        if fed:
                            add_out(q)

                    for_pairs(dve, body)
                    for i in range(FT):
                        gate(PAIRS - 1, ("epi", PAIRS), i)
                    add_out(PAIRS - 1)

                @block.gpsimd
                def _(pool):
                    def residual(q, last):
                        pool.wait_ge(out_stored.sem, out_stored.at(last, 16))
                        pool.tensor_tensor(x3b[:], L.xo[:], brow[:, 2:3, :].broadcast_to([N, 2, D]), ALU.add).then_inc(x3b_done.sem, 1)

                    def lower(q, tiles):
                        for i in tiles:
                            pool.wait_ge(u_hi.sem, u_hi.at(q, i + 1))
                            pool.tensor_tensor(r32(uT[:, i % UR, 1, :]), uf[:, i % 2, :], uT[:, i % UR, 0, :],
                                               ALU.subtract).then_inc(u_lo.sem, 1)

                    for b in range(2):
                        pool.memset(kc[b][STACK:STACK + 2], 1.0).then_inc(ones_done.sem, 1)
                        pool.wait_ge(ones_done.sem, b + 1)

                    def body(p, at, fed, stage):
                        q = before(p)
                        if fed:
                            residual(q, (p, -2))
                        bias_add(pool, L, p, 1)
                        if fed:
                            lower(q, range(EARLY))
                        if stage:
                            ln_rstd(pool, ln2, (p, 1), 0, range(2))
                        if fed:
                            lower(q, range(EARLY, EARLY + 2))
                        if stage:
                            ln_lo(pool, L, ln2, at, ("h0", "h1"), L.hT)
                            parts_pool(pool, L, (p, 1), units_q)
                        ln_rstd(pool, ln3, p, 0, range(1))
                        if fed:
                            lower(q, range(EARLY + 2, FT - 1))
                        ln_rstd(pool, ln3, p, 1, range(1, 2))
                        if fed:
                            lower(q, range(FT - 1, FT))
                        ln_lo(pool, L, ln3, at, ("g0", "g1"), h3T)

                    for_pairs(pool, body)
                    residual(PAIRS - 1, PAIRS - 2)
                    lower(PAIRS - 1, range(FT))


def kernel(**inputs):
    import numpy as np
    import concourse.bacc as bacc
    from concourse.bass_utils import run_bass_kernel_spmd

    a = {n.replace("L0_xattn_", ""): np.asarray(v) for n, v in inputs.items()}

    def columns(v):
        return np.stack([v[0:128], v[128:256], np.concatenate([v[256:320], v[256:320]])], axis=1)

    ln_cols = np.stack([np.stack([columns(a[f"n{i}_g"]), columns(a[f"n{i}_b"])], axis=2) for i in (1, 2, 3)], axis=1)
    arrays = {
        "x": a["x"],
        "ctx_t": np.ascontiguousarray(a["ctx_768"].transpose(0, 2, 1)),
        **{n: a[n] for n in ("q1", "k1", "v1", "o1_w", "q2", "k2", "v2", "o2_w", "ff_w1", "ff_w2")},
        "ln_cols": np.ascontiguousarray(ln_cols.reshape(128, -1)),
        "b1_cols": np.ascontiguousarray(a["ff_b1"].reshape(2 * FT, 128).T),
        "bias_rows": np.ascontiguousarray(np.broadcast_to(
            np.concatenate([a["o1_b"], a["o2_b"], a["ff_b2"]])[None], (N, 3 * D))),
        "ident": np.eye(128, dtype=np.float32),
    }
    nc = bacc.Bacc("TRN2", target_bir_lowering=False, num_devices=1)
    args = [nc.dram_tensor(f"in_{n}", v.shape, mybir.dt.from_np(v.dtype), kind="ExternalInput").ap()
            for n, v in arrays.items()]
    out = nc.dram_tensor("out_0", (B, N, D), F32, kind="ExternalOutput").ap()
    build(nc, *args, out)
    r = run_bass_kernel_spmd(nc, [{f"in_{n}": v for n, v in arrays.items()}], core_ids=[0])
    return r.results[0]["out_0"]
```
